# Optimizing a Trainium2 kernel written in Bass

```python
import numpy as np
import jax
import jax.numpy as jnp

def _softmax(x, axis=-1):
    return jax.nn.softmax(x, axis=axis)

def _gelu(x):
    return jax.nn.gelu(x, approximate=True)

def _silu(x):
    return jax.nn.silu(x)

def _sigmoid(x):
    return jax.nn.sigmoid(x)

def _layernorm(x, axis=-1, eps=1e-05):
    m = jnp.mean(x, axis=axis, keepdims=True)
    v = jnp.var(x, axis=axis, keepdims=True)
    return (x - m) / jnp.sqrt(v + eps)

def _scatter_add(tgt, idx, src, axis=0):
    return tgt.at[idx].add(src)

def _segment_sum(src, seg, n):
    return jax.ops.segment_sum(src, seg, n)
kernel_name = 'mk_flamingo_gated_d2_seqx_r8_3cdee5'

def setup_inputs(seed: int=0):
    np.random.seed(seed)
    _w = jnp.asarray

    def _rec_inputs():
        import jax
        import jax.numpy as jnp
        _rk = jax.random.key(seed)
        x = -0.0003929 + 0.9999 * jax.random.normal(jax.random.fold_in(_rk, 1), (8, 128, 128), jnp.float32)
        _lenS = 128 - jax.random.randint(jax.random.fold_in(_rk, 7), (8,), 0, max(1, 128 // 4) + 1, jnp.int32)
        _lenS2 = 128 - jax.random.randint(jax.random.fold_in(_rk, 8), (8,), 0, max(1, 128 // 4) + 1, jnp.int32)
        _ctx_1024P = jax.random.normal(jax.random.fold_in(_rk, 11), (8, 16, 128), jnp.float32)
        _ctx_1024c = jax.random.dirichlet(jax.random.fold_in(_rk, 511), 0.3 * jnp.ones((16,), jnp.float32), (8, 128))
        _ctx_1024t = jnp.einsum('bsk,bkd->bsd', _ctx_1024c, _ctx_1024P)
        _ctx_1024t = _ctx_1024t * jax.lax.rsqrt(jnp.mean(jnp.square(_ctx_1024t)) + 1e-12) * 0.953939
        ctx_1024 = 2.81802e-05 + 1.00001 * (_ctx_1024t + 0.3 * jax.random.normal(jax.random.fold_in(_rk, 611), (8, 128, 128), jnp.float32))
        _g = jax.random.normal(jax.random.fold_in(_rk, 9001), (2, 2), jnp.float32)
        _g = jnp.sign(_g) * jnp.maximum(jnp.abs(_g), 1.0) + (_g == 0) * 1.0
        g_xattn = _g[0]
        g_ffn = _g[1]
        return (x, ctx_1024, g_xattn, g_ffn)
    x, ctx_1024, g_xattn, g_ffn = _rec_inputs()

    def _L0_xattn_setup():
        import jax, jax.numpy as jnp
        import numpy as np
        B_SZ, T_LEN, C_DIM = (4, 512, 128)

        def _wkv_scan(ek, v, ew):

            def step(carry, xt):
                A, Bd = carry
                ekt, vt = xt
                out = (A, Bd)
                A2 = ew * A + ekt * vt
                B2 = ew * Bd + ekt
                return ((A2, B2), out)
            init = (jnp.zeros_like(ek[:, 0]), jnp.zeros_like(ek[:, 0]))
            xs = (jnp.moveaxis(ek, 1, 0), jnp.moveaxis(v, 1, 0))
            _, (A, Bd) = jax.lax.scan(step, init, xs)
            return (jnp.moveaxis(A, 0, 1), jnp.moveaxis(Bd, 0, 1))

        def _birwkv(r, k, v, w, u):
            wc = w.reshape(-1)
            uc = u.reshape(-1)
            ew = jnp.exp(wc)
            ek = jnp.exp(k)
            Af, Bf = _wkv_scan(ek, v, ew)
            Ab, Bb = _wkv_scan(ek[:, ::-1], v[:, ::-1], ew)
            Ab = Ab[:, ::-1]
            Bb = Bb[:, ::-1]
            cur = jnp.exp(uc + k)
            wkv = (Af + Ab + cur * v) / (Bf + Bb + cur)
            return jax.nn.sigmoid(r) * wkv
        key = jax.random.key(seed)
        k1, k2, k3, k4, k5 = jax.random.split(key, 5)
        r = jax.random.normal(k1, (B_SZ, T_LEN, C_DIM), dtype=jnp.float32)
        k = jax.random.normal(k2, (B_SZ, T_LEN, C_DIM), dtype=jnp.float32)
        v = jax.random.normal(k3, (B_SZ, T_LEN, C_DIM), dtype=jnp.float32)
        w = -(0.3 + jax.random.uniform(k4, (1, 1, C_DIM), dtype=jnp.float32))
        u = jax.random.normal(k5, (1, 1, C_DIM), dtype=jnp.float32) * 0.1
        return {'r': r, 'k': k, 'v': v, 'w': w, 'u': u}
    _L0_xattn_all = _L0_xattn_setup()
    _L0_xattn_in = {k: v for k, v in _L0_xattn_all.items() if k in ('w', 'u')}
    del _L0_xattn_all

    def _L0_ffn_setup():
        import jax, jax.numpy as jnp
        import numpy as np
        B, S = (4, 256)
        D_MODEL, D_FF, N_EXPERTS, TOP_K = (128, 512, 8, 2)
        T = B * S
        CAPACITY_FACTOR, MIN_CAP = (1.25, 4)
        CAP = max(int(CAPACITY_FACTOR * (T * TOP_K / N_EXPERTS)), MIN_CAP)
        key = jax.random.key(seed)
        ks = jax.random.split(key, 6)

        def w(k, shape, fan):
            return jax.random.normal(k, shape, jnp.float32) * fan ** (-0.5)
        return {'x': jax.random.normal(ks[0], (B, S, D_MODEL), jnp.float32), 'Wr': w(ks[1], (D_MODEL, N_EXPERTS), D_MODEL), 'W1': w(ks[2], (N_EXPERTS, D_MODEL, D_FF), D_MODEL), 'b1': jnp.zeros((N_EXPERTS, D_FF), jnp.float32), 'W2': w(ks[3], (N_EXPERTS, D_FF, D_MODEL), D_FF), 'b2': jnp.zeros((N_EXPERTS, D_MODEL), jnp.float32), 'fw1': w(ks[4], (D_MODEL, D_FF), D_MODEL), 'fb1': jnp.zeros((D_FF,), jnp.float32), 'fw2': w(ks[5], (D_FF, D_MODEL), D_FF), 'fb2': jnp.zeros((D_MODEL,), jnp.float32)}
    _L0_ffn_all = _L0_ffn_setup()
    _L0_ffn_in = {k: v for k, v in _L0_ffn_all.items() if k in ('Wr', 'W1', 'b1', 'W2', 'b2', 'fw1', 'fb1', 'fw2', 'fb2')}
    del _L0_ffn_all

    def _L1_xattn_setup():
        import jax, jax.numpy as jnp
        import numpy as np
        D_MODEL = 128
        NUM_HEADS = 16
        HEAD_DIM = D_MODEL // NUM_HEADS
        BATCH = 8
        SEQ = 256
        LN_EPS = 1e-05
        rng = jax.random.key(seed)
        ks = jax.random.split(rng, 16)
        s = 0.02
        w = lambda k: jax.random.normal(k, (D_MODEL, D_MODEL), jnp.float32) * s
        return {'query': jax.random.normal(ks[0], (BATCH, SEQ, D_MODEL), jnp.float32), 'key': jax.random.normal(ks[1], (BATCH, SEQ, D_MODEL), jnp.float32), 'value': jax.random.normal(ks[2], (BATCH, SEQ, D_MODEL), jnp.float32), 'Wq': w(ks[3]), 'bq': jnp.zeros((D_MODEL,), jnp.float32), 'Wk': w(ks[4]), 'bk': jnp.zeros((D_MODEL,), jnp.float32), 'Wv': w(ks[5]), 'bv': jnp.zeros((D_MODEL,), jnp.float32), 'ln_g': jnp.ones((D_MODEL,), jnp.float32), 'ln_b': jnp.zeros((D_MODEL,), jnp.float32), 'Wo': w(ks[6]), 'bo': jnp.zeros((D_MODEL,), jnp.float32)}
    _L1_xattn_all = _L1_xattn_setup()
    _L1_xattn_in = {k: v for k, v in _L1_xattn_all.items() if k in ('Wq', 'bq', 'Wk', 'bk', 'Wv', 'bv', 'ln_g', 'ln_b', 'Wo', 'bo')}
    del _L1_xattn_all

    def _L1_ffn_setup():
        import jax, jax.numpy as jnp
        import numpy as np
        LORA_DIM = 16
        LORA_TOKEN_INDEX = 1
        B, S, D, H = (4, 256, 128, 512)
        key = jax.random.key(seed)
        ks = jax.random.split(key, 6)
        x = jax.random.normal(ks[0], (B, S, D), dtype=jnp.float32)
        W1 = jax.random.normal(ks[1], (H, D), dtype=jnp.float32) * 0.02
        b1 = jnp.zeros((H,), dtype=jnp.float32)
        W2 = jax.random.normal(ks[2], (D, H), dtype=jnp.float32) * 0.02
        b2 = jnp.zeros((D,), dtype=jnp.float32)
        scale = jnp.asarray(0.001, dtype=jnp.float32)
        return {'x': x, 'W1': W1, 'b1': b1, 'W2': W2, 'b2': b2, 'scale': scale}
    _L1_ffn_all = _L1_ffn_setup()
    _L1_ffn_in = {k: v for k, v in _L1_ffn_all.items() if k in ('W1', 'b1', 'W2', 'b2', 'scale')}
    del _L1_ffn_all
    return {'x': x, 'ctx_1024': ctx_1024, 'g_xattn': g_xattn, 'g_ffn': g_ffn, 'L0_xattn_w': _L0_xattn_in['w'], 'L0_xattn_u': _L0_xattn_in['u'], 'L0_ffn_Wr': _L0_ffn_in['Wr'], 'L0_ffn_W1': _L0_ffn_in['W1'], 'L0_ffn_b1': _L0_ffn_in['b1'], 'L0_ffn_W2': _L0_ffn_in['W2'], 'L0_ffn_b2': _L0_ffn_in['b2'], 'L0_ffn_fw1': _L0_ffn_in['fw1'], 'L0_ffn_fb1': _L0_ffn_in['fb1'], 'L0_ffn_fw2': _L0_ffn_in['fw2'], 'L0_ffn_fb2': _L0_ffn_in['fb2'], 'L1_xattn_Wq': _L1_xattn_in['Wq'], 'L1_xattn_bq': _L1_xattn_in['bq'], 'L1_xattn_Wk': _L1_xattn_in['Wk'], 'L1_xattn_bk': _L1_xattn_in['bk'], 'L1_xattn_Wv': _L1_xattn_in['Wv'], 'L1_xattn_bv': _L1_xattn_in['bv'], 'L1_xattn_ln_g': _L1_xattn_in['ln_g'], 'L1_xattn_ln_b': _L1_xattn_in['ln_b'], 'L1_xattn_Wo': _L1_xattn_in['Wo'], 'L1_xattn_bo': _L1_xattn_in['bo'], 'L1_ffn_W1': _L1_ffn_in['W1'], 'L1_ffn_b1': _L1_ffn_in['b1'], 'L1_ffn_W2': _L1_ffn_in['W2'], 'L1_ffn_b2': _L1_ffn_in['b2'], 'L1_ffn_scale': _L1_ffn_in['scale']}

def reference(x, ctx_1024, g_xattn, g_ffn, L0_xattn_w, L0_xattn_u, L0_ffn_Wr, L0_ffn_W1, L0_ffn_b1, L0_ffn_W2, L0_ffn_b2, L0_ffn_fw1, L0_ffn_fb1, L0_ffn_fw2, L0_ffn_fb2, L1_xattn_Wq, L1_xattn_bq, L1_xattn_Wk, L1_xattn_bk, L1_xattn_Wv, L1_xattn_bv, L1_xattn_ln_g, L1_xattn_ln_b, L1_xattn_Wo, L1_xattn_bo, L1_ffn_W1, L1_ffn_b1, L1_ffn_W2, L1_ffn_b2, L1_ffn_scale):
    import jax
    import jax.numpy as jnp

    def _L0_xattn_ref(r, k, v, w, u):
        import jax, jax.numpy as jnp
        import numpy as np
        B_SZ, T_LEN, C_DIM = (4, 512, 128)

        def _wkv_scan(ek, v, ew):

            def step(carry, xt):
                A, Bd = carry
                ekt, vt = xt
                out = (A, Bd)
                A2 = ew * A + ekt * vt
                B2 = ew * Bd + ekt
                return ((A2, B2), out)
            init = (jnp.zeros_like(ek[:, 0]), jnp.zeros_like(ek[:, 0]))
            xs = (jnp.moveaxis(ek, 1, 0), jnp.moveaxis(v, 1, 0))
            _, (A, Bd) = jax.lax.scan(step, init, xs)
            return (jnp.moveaxis(A, 0, 1), jnp.moveaxis(Bd, 0, 1))

        def _birwkv(r, k, v, w, u):
            wc = w.reshape(-1)
            uc = u.reshape(-1)
            ew = jnp.exp(wc)
            ek = jnp.exp(k)
            Af, Bf = _wkv_scan(ek, v, ew)
            Ab, Bb = _wkv_scan(ek[:, ::-1], v[:, ::-1], ew)
            Ab = Ab[:, ::-1]
            Bb = Bb[:, ::-1]
            cur = jnp.exp(uc + k)
            wkv = (Af + Ab + cur * v) / (Bf + Bb + cur)
            return jax.nn.sigmoid(r) * wkv
        return _birwkv(r, k, v, w, u)

    def _L0_ffn_ref(x, Wr, W1, b1, W2, b2, fw1, fb1, fw2, fb2):
        import jax, jax.numpy as jnp
        import numpy as np
        B, S = (4, 256)
        D_MODEL, D_FF, N_EXPERTS, TOP_K = (128, 512, 8, 2)
        T = B * S
        CAPACITY_FACTOR, MIN_CAP = (1.25, 4)
        CAP = max(int(CAPACITY_FACTOR * (T * TOP_K / N_EXPERTS)), MIN_CAP)
        Bx, Sx, D = x.shape
        Tn = Bx * Sx
        xf = x.reshape(Tn, D)
        logits = xf @ Wr
        probs = jax.nn.softmax(logits, axis=-1)
        scores, experts = jax.lax.top_k(probs, TOP_K)
        scores = scores / jnp.maximum(scores.sum(-1, keepdims=True), 1e-09)
        y_fb = jax.nn.gelu(xf @ fw1 + fb1, approximate=False) @ fw2 + fb2
        y = jnp.zeros_like(xf)
        fb_mask = jnp.zeros((Tn,), bool)
        for e in range(N_EXPERTS):
            assign = experts == e
            w_e = jnp.where(assign, scores, 0.0).sum(-1)
            eligible = assign.any(-1) & ~fb_mask
            rank = jnp.cumsum(eligible.astype(jnp.int32)) - 1
            keep = eligible & (rank < CAP)
            overflow = eligible & ~keep
            fb_mask = fb_mask | overflow
            y = jnp.where(overflow[:, None], y_fb, y)
            idx = jnp.nonzero(keep, size=CAP, fill_value=0)[0]
            valid = jnp.arange(CAP) < keep.sum()
            h = jax.nn.gelu(xf[idx] @ W1[e] + b1[e], approximate=False)
            y_e = h @ W2[e] + b2[e]
            y = y.at[idx].add(y_e * (w_e[idx] * valid)[:, None])
        return y.reshape(Bx, Sx, D)

    def _L1_xattn_ref(query, key, value, Wq, bq, Wk, bk, Wv, bv, ln_g, ln_b, Wo, bo):
        import jax, jax.numpy as jnp
        import numpy as np
        D_MODEL = 128
        NUM_HEADS = 16
        HEAD_DIM = D_MODEL // NUM_HEADS
        BATCH = 8
        SEQ = 256
        LN_EPS = 1e-05
        N, L, dm = query.shape
        H, Dh = (NUM_HEADS, HEAD_DIM)
        q = (query @ Wq.T + bq).reshape(N, L, H, Dh).transpose(0, 2, 1, 3)
        k = (key @ Wk.T + bk).reshape(N, L, H, Dh).transpose(0, 2, 1, 3)
        v = (value @ Wv.T + bv).reshape(N, L, H, Dh).transpose(0, 2, 1, 3)
        energy = jnp.einsum('nhld,ngld->nlhg', q, k)
        attn = jax.nn.softmax(energy / jnp.sqrt(jnp.float32(dm)), axis=3)
        out = jnp.einsum('nlhg,ngld->nhld', attn, v)
        out = out.transpose(0, 2, 1, 3).reshape(N, L, dm)
        mu = out.mean(axis=-1, keepdims=True)
        var = out.var(axis=-1, keepdims=True)
        out = (out - mu) / jnp.sqrt(var + LN_EPS) * ln_g + ln_b
        return out @ Wo.T + bo

    def _L1_ffn_ref(x, W1, b1, W2, b2, scale):
        import jax, jax.numpy as jnp
        import numpy as np
        LORA_DIM = 16
        LORA_TOKEN_INDEX = 1
        B, S, D, H = (4, 256, 128, 512)
        Bx, Sx, Dx = x.shape
        Hx = W1.shape[0]
        lt = jax.lax.dynamic_slice_in_dim(x, LORA_TOKEN_INDEX, LORA_DIM, axis=1)
        even = lt[:, ::2, :]
        odd = lt[:, 1::2, :]
        m1 = (even[:, :4, :, None] * odd[:, :4, None, :]).reshape(Bx, Hx, Dx)
        m2 = (even[:, 4:, :, None] * odd[:, 4:, None, :]).reshape(Bx, Dx, Hx)
        h = jnp.einsum('bsd,hd->bsh', x, W1) + scale * jnp.einsum('bsd,bhd->bsh', x, m1) + b1
        h = jax.nn.gelu(h, approximate=False)
        out = jnp.einsum('bsh,oh->bso', h, W2) + scale * jnp.einsum('bsh,boh->bso', h, m2) + b2
        return out
    x = x + jnp.tanh(g_xattn[0]) * _L0_xattn_ref(_layernorm(x, axis=-1), ctx_1024, ctx_1024, L0_xattn_w, L0_xattn_u)
    x = x + jnp.tanh(g_ffn[0]) * _L0_ffn_ref(_layernorm(x, axis=-1), L0_ffn_Wr, L0_ffn_W1, L0_ffn_b1, L0_ffn_W2, L0_ffn_b2, L0_ffn_fw1, L0_ffn_fb1, L0_ffn_fw2, L0_ffn_fb2)
    x = x + jnp.tanh(g_xattn[1]) * _L1_xattn_ref(_layernorm(x, axis=-1), ctx_1024, ctx_1024, L1_xattn_Wq, L1_xattn_bq, L1_xattn_Wk, L1_xattn_bk, L1_xattn_Wv, L1_xattn_bv, L1_xattn_ln_g, L1_xattn_ln_b, L1_xattn_Wo, L1_xattn_bo)
    x = x + jnp.tanh(g_ffn[1]) * _L1_ffn_ref(_layernorm(x, axis=-1), L1_ffn_W1, L1_ffn_b1, L1_ffn_W2, L1_ffn_b2, L1_ffn_scale)
    return x

_drawn_inputs = setup_inputs


def setup_inputs(seed=0):
    import zlib

    import numpy as np

    out = dict(_drawn_inputs(seed))
    spreads = {'g_ffn': (-1.0, 0.6),
     'L0_ffn_b1': (0.0, 0.1),
     'L0_ffn_b2': (0.0, 0.1),
     'L0_ffn_fb1': (0.0, 0.1),
     'L0_ffn_fb2': (0.0, 0.1),
     'L1_xattn_bq': (0.0, 0.8),
     'L1_xattn_bk': (0.0, 0.8),
     'L1_xattn_bv': (0.0, 0.31),
     'L1_xattn_ln_g': (1.0, 0.2),
     'L1_xattn_ln_b': (0.0, 0.427),
     'L1_xattn_bo': (0.0, 0.1),
     'L1_ffn_b1': (0.0, 0.501),
     'L1_ffn_b2': (0.0, 0.1)}
    factors = {'L0_xattn_u': 3.686, 'L1_xattn_Wq': 8.0, 'L1_xattn_Wk': 8.0}
    for name, (base, spread) in spreads.items():
        noise = np.random.default_rng([zlib.crc32(name.encode()), seed]).standard_normal(out[name].shape)
        drawn = base * np.exp(spread * noise) if base else spread * noise
        out[name] = jnp.asarray(drawn.astype(out[name].dtype))
    for name, factor in factors.items():
        out[name] = (out[name] * factor).astype(out[name].dtype)
    return out
```

```python
from contextlib import ExitStack

import concourse.bass as bass
from concourse import mybir

P = 128
NB = 8
GT = 4
NG = NB // GT
D = 128
FF = 512
FB = FF // P
NE = 8
FALL = NE
NF = NE + 1
CAP = max(int(1.25 * (4 * 256 * 2 / NE)), 4)
NH = 16
DH = D // NH
NL = 4
EPS = 1e-5
SEG = P + 1
SCAN = NB * SEG + 1
NTERM = NF + 1
CHUNK = 4
NWORK = 3
INV_SQRT_D = float(D) ** -0.5

ALU = mybir.AluOpType
ACT = mybir.ActivationFunctionType
F32 = mybir.dt.float32
BF16 = mybir.dt.bfloat16
U32 = mybir.dt.uint32
AX_X = mybir.AxisListType.X

C_W, C_U, C_LNG, C_LNB, C_B1 = 0, 1, 2, 3, 4
C_L1B1 = C_B1 + NF * FB
NCOL = C_L1B1 + FB
S_KV, S_Q, S_O, S_R = 0, 2 * D, 3 * D, 4 * D
NSMALL = 4 * D + NE
R_KV, R_Q, R_O, R_B2 = 0, 2 * D, 3 * D, 4 * D
NROW = 5 * D
G_X0, G_F0, G_X1, G_F1, G_SCALE = range(5)

PIECES = ["stat3", "norm3", "turn3", "query", "eprod", "esum", "vprod", "soft", "vsum", "norm4", "turn4",
          "wo", "norm5", "turn5", "lora", "up1", "low2", "down1"]
LAG = [0, 2, 3, 4, 5, 10, 13, 14, 18, 21, 22, 23, 25, 26, 27, 29, 32, 34]


def timeline():
    items = []
    at = 0.0

    def put(when, *item):
        items.append((when, len(items), item))

    for g, n in ((0, -12), (1, -7)):
        put(n, "mix", g)
    put(-8, "kv", 1)
    put(-13, "kv", 0)
    put(-6, "rows", 0)
    blocks = [("up", 0, e, j) for e in (FALL, *range(NE)) for j in range(FB)]
    for i, b in enumerate(blocks):
        if i == 8:
            put(at, "rows", 1)
        if i == 10:
            put(at, "choose")
        if i >= 13 and (i - 13) % 2 == 0 and (i - 13) // 2 < NE:
            put(at, "rank", (i - 13) // 2)
        if i == 31:
            put(at, "coef")
        put(at, *b)
        at += 1

    def down(t):
        nonlocal at
        for n in range(t * NTERM, (t + 1) * NTERM):
            at += 1
            if (n + 1) % CHUNK == 0:
                put(at, "down", n // CHUNK)
        done = at + -((t + 1) * NTERM) % CHUNK
        for piece, lag in zip(PIECES, LAG):
            put(done + lag + 0.5, piece, t)

    for t in range(GT):
        down(t)
    for e in (FALL, *range(NE)):
        for j in range(FB):
            put(at, "up", 1, e, j)
            at += 1
    for t in range(GT, NB):
        down(t)
    return [item for _, _, item in sorted(items, key=lambda x: x[:2])]


NTH_UP = {(g, e): g * NF + i for g in range(NG) for i, e in enumerate((FALL, *range(NE)))}
TERMS = [(t, e) for t in range(NB) for e in (None, FALL, *range(NE))]
TIMELINE = timeline()
WORK = [("kv", t) if item[0] == "kv" else item for item in TIMELINE if item[0] in ("kv", "up", "down")
        for t in (range(item[1] * GT, item[1] * GT + GT) if item[0] == "kv" else (0,))]


def flamingo_kernel(nc, ctxT, x_in, cols, gates, rows, small, w_up, w_down, b2, l1_up, l1_down, out):
    with ExitStack() as ctx:
        def sb(name, shape, dt=F32):
            return ctx.enter_context(nc.sbuf_tensor(name, shape, dt))

        def bank(name):
            return ctx.enter_context(nc.psum_tensor(name, [P, 512], F32))

        def sem(name):
            return ctx.enter_context(nc.semaphore(name))

        ctxT_sb = sb("ctxT_sb", [P, NB * P])
        x = sb("x", [P, NB, D])
        xn = sb("xn", [P, NB, D])
        col = sb("col", [P, NCOL])
        gate = sb("gate", [P, 5])
        tg = sb("tg", [P, 4])
        row = sb("row", [1, NROW])
        sw = sb("sw", [P, NSMALL])
        wu = sb("wu", [P, NF, FF])
        wd = sb("wd", [P, NF, FB, D])
        b2_sb = sb("b2_sb", [NF, D])
        w1u = sb("w1u", [P, FF])
        w1d = sb("w1d", [P, FB, D])
        ew = sb("ew", [P, 2])
        decay = sb("decay", [P, SCAN])
        src = sb("src", [P, 2, SCAN])
        fwd = sb("fwd", [P, 2, SCAN])
        bwd = sb("bwd", [P, 2, SCAN])
        diag_u = sb("diag_u", [P, P])
        ident = sb("ident", [P, P])
        tri = sb("tri", [P, P], BF16)
        ones_bf = sb("ones_bf", [P, P], BF16)
        ones_row = sb("ones_row", [1, P])
        iota_e = sb("iota_e", [P, NE])
        minus_half = sb("minus_half", [P, NB])
        one8 = sb("one8", [P, NB])
        mask_s = sb("mask_s", [NL, NL, P])
        on = sb("on", [P, NB, D])
        mixed = sb("mixed", [P, GT * D])
        bn = sb("bn", [P, NB, 6])
        mv = sb("mv", [P, 5, NB, 2])
        ve = sb("ve", [P, 5, NB])
        rstd = sb("rstd", [P, 5, NB])
        xnT = sb("xnT", [P, NB, P])
        hid = sb("hid", [P, NF, FB, GT * P])
        k_sb = sb("k_sb", [P, NB, D])
        v_sb = sb("v_sb", [P, NB, D])
        logit = sb("logit", [P, NB, NE])
        top = sb("top", [P, NB, 8])
        topi = sb("topi", [P, NB, 8], U32)
        topf = sb("topf", [P, NB, 2])
        gap = sb("gap", [P, NB])
        egap = sb("egap", [P, NB])
        den2 = sb("den2", [P, NB])
        wt = sb("wt", [P, 2, NB])
        hot = sb("hot", [P, 2, NB, NE])
        assign = sb("assign", [P, NB, NE])
        weight = sb("weight", [P, NB, NE])
        live = sb("live", [P, NB])
        over = sb("over", [P, NB])
        elig = sb("elig", [P, NE, NB], BF16)
        before = sb("before", [P, NE, NB + 1], BF16)
        coef = sb("coef", [P, NB, NF])
        coefT = sb("coefT", [NF, NB, P])
        q_sb = sb("q_sb", [P, 2, D])
        xT3 = sb("xT3", [P, 2, P])
        oT = sb("oT", [P, 2, P])
        xT5 = sb("xT5", [P, 2, P])
        en = sb("en", [P, 2, NH, NH])
        mx = sb("mx", [P, 2, NH])
        pr = sb("pr", [P, 2, NH, NH])
        sm = sb("sm", [P, 2, NH])
        rs = sb("rs", [P, 2, NH])
        att = sb("att", [P, 2, D])
        even1 = sb("even1", [NL, 2, P])
        even2 = sb("even2", [NL, 2, FB, NL, P // NL])
        low = sb("low", [NL, 2, FB, P])

        eprod = [fwd[:, :, :].rearrange("p a s -> p (a s)")[:, 0:NH * NH * DH],
                 bwd[:, :, :].rearrange("p a s -> p (a s)")[:, 0:NH * NH * DH]]
        vprod = src[:, :, :].rearrange("p a s -> p (a s)")[:, 0:NH * NH * DH]
        u_mask = decay[0:NL, 0:2 * NL * P].rearrange("p (i j t) -> p i j t", i=2, j=NL)
        hid1 = ctxT_sb[:, :].rearrange("p (i r t) -> p i r t", i=2, r=FB)

        work = [bank(f"ps_work{i}") for i in range(NWORK)]
        ps_num = bank("ps_num")
        ps_den = bank("ps_den")
        ps_turn = bank("ps_turn")
        ps_logit = bank("ps_logit")
        ps_rank = bank("ps_rank")
        ps_q, ps_o, ps_x5, ps_h1, ps_y = ps_num, ps_den, ps_turn, ps_logit, ps_rank
        T3, Q = ps_q[:, 0:P], ps_q[:, P:2 * P]
        T4, WO = ps_o[:, 0:P], ps_o[:, P:2 * P]
        T5, FAC = ps_x5[:, 0:P], ps_x5[0:NL, P:4 * P]
        Y5 = ps_y[:, 0:D]

        def work_bank(*item):
            return work[WORK.index(item) % NWORK]

        def place(n):
            return work_bank("down", n // CHUNK)[:, n % CHUNK * D:(n % CHUNK + 1) * D]

        def seg(buf, a, g, off):
            v = buf[:, a, off:off + NB * SEG] if off + NB * SEG <= SCAN else None
            return v.rearrange("p (b s) -> p b s", s=SEG)[:, g * GT:(g + 1) * GT, 0:P]

        ld_ctx, ld_x, ld_col, ld_gate, ld_row, ld_small, ld_b2, ld_l1 = (
            sem(f"ld_{n}") for n in ("ctx", "x", "col", "gate", "row", "small", "b2", "l1"))
        ld_up = [sem(f"ld_up{e}") for e in range(NF)]
        ld_dn = [sem(f"ld_dn{e}") for e in range(NF)]
        consts, zeroed, masks, mask_ok = sem("consts"), sem("zeroed"), sem("masks"), sem("mask_ok")
        ew_ok, tg_ok, ek_ok, decay_ok, diag_ok = (sem(n) for n in ("ew_ok", "tg_ok", "ek_ok", "decay_ok", "diag_ok"))
        ekv_ok, scan_ok = sem("ekv_ok"), sem("scan_ok")
        kv_ps, kv_ok = sem("kv_ps"), sem("kv_ok")
        bn_ok, aggr_ok, ve_ok, rstd_ok, norm_ok = ([sem(f"{n}{i}") for i in range(5)] for n in (
            "bn_ok", "aggr_ok", "ve_ok", "rstd_ok", "norm_ok"))
        er_ok, mix_ps, dn_ok, rec_ok, mixed_ok, x1_ok = (
            sem(n) for n in ("er_ok", "mix_ps", "dn_ok", "rec_ok", "mixed_ok", "x1_ok"))
        turn_ps, xnT_ok, logit_ps, logit_ok = (sem(n) for n in ("turn_ps", "xnT_ok", "logit_ps", "logit_ok"))
        ch, egap_ok = sem("choose_step"), sem("egap_ok")
        rk, elig_ok, rank_ps = sem("rank_step"), sem("elig_ok"), sem("rank_ps")
        coef_ok, coefT_ps, coefT_ok = (
            sem(n) for n in ("coef_ok", "coefT_ps", "coefT_ok"))
        up_ps, up_ok, down_ps, sum_ok = (sem(n) for n in ("up_ps", "up_ok", "down_ps", "sum_ok"))
        T3_ps, T3_ok, q_ps, q_ok = (sem(n) for n in ("T3_ps", "T3_ok", "q_ps", "q_ok"))
        eprod_ok, ered_ok, max_ok, sub_ok, exp_ok, vprod_ok, soft_ok, rs_ok, vred_ok, att_ok = (
            sem(n) for n in ("eprod_ok", "ered_ok", "max_ok", "sub_ok", "exp_ok", "vprod_ok", "soft_ok", "rs_ok",
                             "vred_ok", "att_ok"))
        T4_ps, oT_ok, wo_ps, x3_ok, T5_ps, T5_ok = (
            sem(n) for n in ("T4_ps", "oT_ok", "wo_ps", "x3_ok", "T5_ps", "T5_ok"))
        fac_ps, fac_ok, up1_ps, hid1_ok, low_ps, low_ok, y_ps, y_ok, stored = (
            sem(n) for n in ("fac_ps", "fac_ok", "up1_ps", "hid1_ok", "low_ps", "low_ok", "y_ps", "y_ok", "stored"))

        block = ctx.enter_context(nc.Block())

        @block.sync
        def _(sp):
            sp.dma_start(ctxT_sb[:, :], ctxT).then_inc(ld_ctx, 16)
            sp.dma_start(col[:, :], cols).then_inc(ld_col, 16)
            sp.dma_start(x[:, :, :].rearrange("p b d -> p (b d)"), x_in).then_inc(ld_x, 16)
            sp.dma_start(sw[:, :], small).then_inc(ld_small, 16)
            sp.dma_start(row[:, :], rows).then_inc(ld_row, 16)
            sp.dma_start(gate[:, :], gates.broadcast_to([P, 5])).then_inc(ld_gate, 16)
            for e in (FALL, *range(NE)):
                sp.dma_start(wu[:, e, :], w_up[:, e, :]).then_inc(ld_up[e], 16)
            sp.dma_start(b2_sb[:, :], b2).then_inc(ld_b2, 16)
            for e in (FALL, *range(NE)):
                sp.dma_start(wd[:, e, :, :], w_down[:, e, :, :]).then_inc(ld_dn[e], 16)
            sp.dma_start(w1u[:, :], l1_up).then_inc(ld_l1, 16)
            sp.dma_start(w1d[:, :, :], l1_down).then_inc(ld_l1, 16)
            for t in range(NB):
                sp.wait_ge(y_ok, t + 1)
                sp.dma_start(out[t, :, :], x[:, t, :]).then_inc(stored, 16)
            sp.wait_ge(stored, 16 * NB)

        @block.gpsimd
        def _(pool):
            nc.gpsimd.memset(ident[:, :], 0.0).then_inc(zeroed, 1)
            nc.gpsimd.memset(ones_row[:, :], 1.0)
            nc.gpsimd.memset(minus_half[:, :], -0.5)
            nc.gpsimd.memset(one8[:, :], 1.0)
            nc.gpsimd.memset(ones_bf[:, :], 1.0).then_inc(zeroed, 1)
            nc.gpsimd.memset(mask_s[:, :, :], 0.0).then_inc(zeroed, 1)
            pool.wait_ge(zeroed, 3)
            nc.gpsimd.affine_select(out=ident[:, :], in_=ident[:, :], compare_op=ALU.not_equal, fill=1.0, base=0,
                                    pattern=[[-1, P]], channel_multiplier=1)
            nc.gpsimd.affine_select(out=tri[:, :], in_=ones_bf[:, :], compare_op=ALU.is_ge, fill=0.0, base=0,
                                    pattern=[[1, P]], channel_multiplier=-1)
            nc.gpsimd.affine_select(out=mask_s[:, :, :], in_=mask_s[:, :, :], compare_op=ALU.not_equal, fill=1.0,
                                    base=0, pattern=[[-1, NL], [0, P]], channel_multiplier=1)
            nc.gpsimd.iota(iota_e[:, :], [[1, NE]], base=0, channel_multiplier=0,
                           allow_small_or_imprecise_dtypes=True).then_inc(consts, 1)

            def root(i, a, b, count):
                pool.wait_ge(ve_ok[i], count)
                nc.gpsimd.tensor_tensor(rstd[:, i, a:b], ve[:, i, a:b], minus_half[:, 0:b - a],
                                        ALU.pow).then_inc(rstd_ok[i], 1)

            root(0, 0, NB, 1)
            for name, *a in TIMELINE:
                if name == "rows":
                    root(1, GT * a[0], GT * a[0] + GT, a[0] + 1)
                elif name == "stat3":
                    root(2, a[0], a[0] + 1, a[0] + 1)
                elif name == "vsum":
                    root(3, a[0], a[0] + 1, a[0] + 1)
                elif name == "wo":
                    root(4, a[0], a[0] + 1, a[0] + 1)
                elif name == "eprod":
                    t, = a
                    pool.wait_ge(q_ok, t + 1)
                    pool.wait_ge(kv_ok, t + 1)
                    if t >= 2:
                        pool.wait_ge(ered_ok, t - 1)
                    qv = q_sb[:, t % 2, :].rearrange("p (h g d) -> p h g d", h=NH, g=1).broadcast_to([P, NH, NH, DH])
                    kv = k_sb[:, t, :].rearrange("p (h g d) -> p h g d", h=1, g=NH).broadcast_to([P, NH, NH, DH])
                    nc.gpsimd.tensor_tensor(eprod[t % 2].rearrange("p (h g d) -> p h g d", h=NH, g=NH), qv, kv,
                                            ALU.mult).then_inc(eprod_ok, 1)
                elif name == "vprod":
                    t, = a
                    pool.wait_ge(exp_ok, t + 1)
                    if t >= 1:
                        pool.wait_ge(vred_ok, t)
                    pv = pr[:, t % 2, :, :].unsqueeze(2).broadcast_to([P, NH, DH, NH])
                    vv = v_sb[:, t, :].rearrange("p (h d g) -> p h d g", h=1, g=NH).broadcast_to([P, NH, DH, NH])
                    nc.gpsimd.tensor_tensor(vprod.rearrange("p (h d g) -> p h d g", h=NH, d=DH), pv, vv,
                                            ALU.mult).then_inc(vprod_ok, 1)

        @block.scalar
        def _(act):
            act.wait_ge(ld_col, 16)
            nc.scalar.activation(ew[:, :], col[:, C_W:C_U + 1], ACT.Exp).then_inc(ew_ok, 1)
            act.wait_ge(ld_ctx, 16)
            for g in range(NG):
                nc.scalar.activation(seg(src, 1, g, 1),
                                     ctxT_sb[:, :].rearrange("p (b s) -> p b s", s=P)[:, g * GT:(g + 1) * GT, :],
                                     ACT.Exp).then_inc(ek_ok, 1)
            act.wait_ge(ld_gate, 16)
            nc.scalar.activation(tg[:, :], gate[:, 0:4], ACT.Tanh).then_inc(tg_ok, 1)
            act.wait_ge(norm_ok[0], 1)
            nc.scalar.activation(on[:, :, :], xn[:, :, :], ACT.Exp, scale=-1.0).then_inc(er_ok, 1)
            for name, *a in TIMELINE:
                if name == "kv":
                    for t in range(a[0] * GT, a[0] * GT + GT):
                        act.wait_ge(kv_ps, t + 1)
                        nc.scalar.copy(k_sb[:, t, :], work_bank("kv", t)[:, 0:D])
                        nc.scalar.copy(v_sb[:, t, :], work_bank("kv", t)[:, D:2 * D]).then_inc(kv_ok, 1)
                elif name == "rows":
                    g, = a
                    act.wait_ge(turn_ps, g + 1)
                    nc.scalar.copy(xnT[:, g * GT:(g + 1) * GT, :].rearrange("p b t -> p (b t)"),
                                   ps_turn[:, :]).then_inc(xnT_ok, 1)
                elif name == "choose":
                    act.wait_ge(ch, 3)
                    nc.scalar.activation(egap[:, :], gap[:, :], ACT.Exp).then_inc(egap_ok, 1)
                elif name == "up":
                    g, e, j = a
                    n = NTH_UP[g, e] * FB + j
                    act.wait_ge(up_ps, n + 1)
                    if g:
                        act.wait_ge(down_ps, TERMS.index((GT - 1, e)) // CHUNK + 1)
                    nc.scalar.activation(hid[:, e, j, :], work_bank("up", g, e, j)[:, :], ACT.Gelu,
                                         bias=col[:, C_B1 + e * FB + j:C_B1 + e * FB + j + 1]).then_inc(up_ok, 1)
                elif name == "turn3":
                    t, = a
                    act.wait_ge(T3_ps, t + 1)
                    if t >= 2:
                        act.wait_ge(q_ps, t - 1)
                    nc.scalar.copy(xT3[:, t % 2, :], T3).then_inc(T3_ok, 1)
                elif name == "query":
                    t, = a
                    act.wait_ge(q_ps, t + 1)
                    if t >= 2:
                        act.wait_ge(eprod_ok, t - 1)
                    nc.scalar.copy(q_sb[:, t % 2, :], Q).then_inc(q_ok, 1)
                elif name == "esum":
                    t, = a
                    act.wait_ge(sub_ok, t + 1)
                    if t >= 2:
                        act.wait_ge(vprod_ok, t - 1)
                        act.wait_ge(soft_ok, t - 1)
                    nc.scalar.activation(pr[:, t % 2, :, :], en[:, t % 2, :, :], ACT.Exp,
                                         scale=INV_SQRT_D).then_inc(exp_ok, 1)
                elif name == "turn5":
                    t, = a
                    act.wait_ge(T5_ps, t + 1)
                    if t >= 2:
                        act.wait_ge(low_ps, t - 1)
                    nc.scalar.copy(xT5[:, t % 2, :], T5).then_inc(T5_ok, 1)
                elif name == "up1":
                    t, = a
                    act.wait_ge(up1_ps, t + 1)
                    if t >= 2:
                        act.wait_ge(y_ps, t - 1)
                    for j in range(FB):
                        last = nc.scalar.activation(hid1[:, t % 2, j, :], ps_h1[:, j * P:(j + 1) * P], ACT.Gelu,
                                                    bias=col[:, C_L1B1 + j:C_L1B1 + j + 1])
                    last.then_inc(hid1_ok, 1)
                elif name == "low2":
                    t, = a
                    act.wait_ge(low_ps, t + 1)
                    if t >= 2:
                        act.wait_ge(y_ps, t - 1)
                    nc.scalar.copy(low[:, t % 2, :, :].rearrange("p r t -> p (r t)"),
                                   ps_h1[0:NL, :]).then_inc(low_ok, 1)

        @block.vector
        def _(dve):
            def stats(i, tiles, source, ready, count):
                if ready is not None:
                    dve.wait_ge(ready, count)
                for t in tiles:
                    last = nc.vector.bn_stats(bn[:, t, :], source(t))
                last.then_inc(bn_ok[i], 1)
                call = tiles[0] // len(tiles) + 1
                dve.wait_ge(bn_ok[i], call)
                for t in tiles:
                    last = nc.vector.bn_aggr(mv[:, i, t, :], bn[:, t, :])
                last.then_inc(aggr_ok[i], 1)
                dve.wait_ge(aggr_ok[i], call)
                a, b = tiles[0], tiles[-1] + 1
                nc.vector.tensor_scalar(ve[:, i, a:b], mv[:, i, a:b, 1], EPS, None, ALU.add).then_inc(ve_ok[i], 1)

            def norm(i, tiles, source, target):
                dve.wait_ge(rstd_ok[i], tiles[0] // len(tiles) + 1)
                for t in tiles:
                    last = nc.vector.tensor_scalar(target(t), source(t), mv[:, i, t, 0:1], rstd[:, i, t:t + 1],
                                                   ALU.subtract, ALU.mult)
                last.then_inc(norm_ok[i], 1)

            def x_tile(t):
                return x[:, t, :]

            def xn_tile(t):
                return xn[:, t, :]

            nc.vector.memset(decay[:, :], 1.0)
            nc.vector.memset(src[:, :, 0:SCAN:SEG], 0.0)
            nc.vector.memset(live[:, :], 1.0)
            nc.vector.memset(before[:, :, 0:1], 0.0).then_inc(masks, 1)
            dve.wait_ge(masks, 1)
            nc.vector.memset(decay[:, 0:SCAN:SEG], 0.0).then_inc(masks, 1)
            dve.wait_ge(masks, 2)
            dve.wait_ge(ew_ok, 1)
            nc.vector.tensor_scalar(decay[:, :], decay[:, :], ew[:, 0:1], None, ALU.mult).then_inc(decay_ok, 1)
            dve.wait_ge(consts, 1)
            nc.vector.tensor_scalar(diag_u[:, :], ident[:, :], ew[:, 1:2], None, ALU.mult).then_inc(diag_ok, 1)
            dve.wait_ge(decay_ok, 1)

            def scans(g):
                dve.wait_ge(ek_ok, g + 1)
                nc.vector.tensor_tensor(seg(src, 0, g, 1), seg(src, 1, g, 1),
                                        ctxT_sb[:, :].rearrange("p (b s) -> p b s", s=P)[:, g * GT:(g + 1) * GT, :],
                                        ALU.mult).then_inc(ekv_ok, 1)
                a, b = g * GT * SEG, (g + 1) * GT * SEG
                back = slice(b, a, -1)
                for s in (1, 0):
                    if s == 0:
                        dve.wait_ge(ekv_ok, g + 1)
                    nc.vector.tensor_tensor_scan(fwd[:, s, a:b], decay[:, a:b], src[:, s, a:b], 0.0,
                                                 ALU.mult, ALU.add)
                    last = nc.vector.tensor_tensor_scan(bwd[:, s, back], decay[:, back], src[:, s, back], 0.0,
                                                        ALU.mult, ALU.add)
                last.then_inc(scan_ok, 1)

            def mixer(g):
                ts = slice(g * GT, (g + 1) * GT)
                dve.wait_ge(mix_ps, g + 1)
                dve.wait_ge(er_ok, 1)
                dve.wait_ge(tg_ok, 1)
                if g:
                    dve.wait_ge(x1_ok, g)
                nc.vector.scalar_tensor_tensor(mixed[:, :], on[:, ts, :].rearrange("p b d -> p (b d)"), 1.0,
                                               ps_den[:, :], ALU.add, ALU.mult).then_inc(dn_ok, 1)
                dve.wait_ge(dn_ok, g + 1)
                nc.vector.reciprocal(mixed[:, :], mixed[:, :]).then_inc(rec_ok, 1)
                dve.wait_ge(rec_ok, g + 1)
                nc.vector.scalar_tensor_tensor(mixed[:, :], ps_num[:, :], tg[:, G_X0:G_X0 + 1], mixed[:, :],
                                               ALU.mult, ALU.mult).then_inc(mixed_ok, 1)
                dve.wait_ge(mixed_ok, g + 1)
                xg = x[:, ts, :].rearrange("p b d -> p (b d)")
                nc.vector.tensor_tensor(xg, xg, mixed[:, :], ALU.add).then_inc(x1_ok, 1)

            scans(0)
            dve.wait_ge(ld_x, 16)
            stats(0, list(range(NB)), x_tile, None, 0)
            norm(0, list(range(NB)), x_tile, xn_tile)

            for name, *a in TIMELINE:
                if name == "mix":
                    mixer(a[0])
                    if a[0] == 0:
                        scans(1)
                elif name == "rows":
                    g, = a
                    tiles = list(range(g * GT, g * GT + GT))
                    stats(1, tiles, x_tile, x1_ok, g + 1)
                    norm(1, tiles, x_tile, xn_tile)
                elif name == "choose":
                    dve.wait_ge(logit_ps, NG)
                    nc.vector.tensor_copy(logit[:, :, :].rearrange("p b e -> p (b e)"),
                                          ps_logit[:, 0:NB * NE]).then_inc(logit_ok, 1)
                    dve.wait_ge(logit_ok, 1)
                    for t in range(NB):
                        last = nc.vector.max(top[:, t, :], logit[:, t, :])
                    last.then_inc(ch, 1)
                    dve.wait_ge(ch, 1)
                    for t in range(NB):
                        last = nc.vector.max_index(topi[:, t, :], top[:, t, :], logit[:, t, :])
                    last.then_inc(ch, 1)
                    nc.vector.tensor_tensor(gap[:, :], top[:, :, 1], top[:, :, 0], ALU.subtract).then_inc(ch, 1)
                    dve.wait_ge(ch, 3)
                    nc.vector.tensor_copy(topf[:, :, :], topi[:, :, 0:2]).then_inc(ch, 1)
                    dve.wait_ge(ch, 4)
                    dve.wait_ge(consts, 1)
                    for i in range(2):
                        last = nc.vector.tensor_tensor(
                            hot[:, i, :, :], iota_e[:, :].unsqueeze(1).broadcast_to([P, NB, NE]),
                            topf[:, :, i:i + 1].broadcast_to([P, NB, NE]), ALU.is_equal)
                    last.then_inc(ch, 1)
                    dve.wait_ge(ch, 5)
                    nc.vector.tensor_tensor(assign[:, :, :], hot[:, 0, :, :], hot[:, 1, :, :],
                                            ALU.add).then_inc(ch, 1)
                    dve.wait_ge(egap_ok, 1)
                    nc.vector.tensor_scalar(den2[:, :], egap[:, :], 1.0, None, ALU.add).then_inc(ch, 1)
                    dve.wait_ge(ch, 7)
                    nc.vector.reciprocal(wt[:, 0, :], den2[:, :]).then_inc(ch, 1)
                    dve.wait_ge(ch, 8)
                    nc.vector.tensor_tensor(wt[:, 1, :], wt[:, 0, :], egap[:, :], ALU.mult).then_inc(ch, 1)
                    dve.wait_ge(ch, 9)
                    for i in range(2):
                        last = nc.vector.tensor_tensor(
                            hot[:, i, :, :], hot[:, i, :, :],
                            wt[:, i, :].unsqueeze(2).broadcast_to([P, NB, NE]), ALU.mult)
                    last.then_inc(ch, 1)
                    dve.wait_ge(ch, 10)
                    nc.vector.tensor_tensor(weight[:, :, :], hot[:, 0, :, :], hot[:, 1, :, :],
                                            ALU.add).then_inc(ch, 1)
                    dve.wait_ge(ch, 11)
                    dve.wait_ge(tg_ok, 1)
                    nc.vector.tensor_scalar(weight[:, :, :], weight[:, :, :], tg[:, G_F0:G_F0 + 1], None,
                                            ALU.mult).then_inc(ch, 1)
                    dve.wait_ge(ch, 12)
                elif name == "rank":
                    e, = a
                    dve.wait_ge(rk, 2 * e) if e else dve.wait_ge(masks, 2)
                    nc.vector.tensor_tensor(elig[:, e, :], assign[:, :, e], live[:, :], ALU.mult).then_inc(elig_ok, 1)
                    dve.wait_ge(elig_ok, 2 * e + 1)
                    nc.vector.tensor_tensor_scan(before[:, e, 1:NB + 1], one8[:, :], elig[:, e, :], 0.0,
                                                 ALU.mult, ALU.add).then_inc(elig_ok, 1)
                    dve.wait_ge(rank_ps, e + 1)
                    nc.vector.scalar_tensor_tensor(over[:, :], ps_rank[:, e * NB:(e + 1) * NB],
                                                   float(CAP), elig[:, e, :], ALU.is_gt, ALU.mult).then_inc(rk, 1)
                    dve.wait_ge(rk, 2 * e + 1)
                    nc.vector.tensor_tensor(live[:, :], live[:, :], over[:, :], ALU.subtract).then_inc(rk, 1)
                elif name == "coef":
                    dve.wait_ge(rk, 2 * NE)
                    nc.vector.tensor_tensor(coef[:, :, 0:NE], weight[:, :, :],
                                            live[:, :].unsqueeze(2).broadcast_to([P, NB, NE]), ALU.mult)
                    nc.vector.tensor_scalar(over[:, :], live[:, :], -1.0, 1.0, ALU.mult, ALU.add).then_inc(rk, 1)
                    dve.wait_ge(rk, 2 * NE + 1)
                    nc.vector.tensor_scalar(coef[:, :, FALL], over[:, :], tg[:, G_F0:G_F0 + 1], None,
                                            ALU.mult).then_inc(coef_ok, 1)
                    for g in range(NG):
                        dve.wait_ge(coefT_ps, g + 1)
                        nc.vector.tensor_copy(coefT[:, g * GT:(g + 1) * GT, :].rearrange("p b t -> p (b t)"),
                                              ps_turn[0:NF, :]).then_inc(coefT_ok, 1)
                elif name == "down":
                    c, = a
                    dve.wait_ge(down_ps, c + 1)
                    dve.wait_ge(coef_ok, 1)
                    for n in range(c * CHUNK, (c + 1) * CHUNK):
                        t, e = TERMS[n]
                        if n:
                            dve.wait_ge(sum_ok, n)
                        nc.vector.scalar_tensor_tensor(x[:, t, :], place(n),
                                                       1.0 if e is None else coef[:, t, e:e + 1], x[:, t, :],
                                                       ALU.mult, ALU.add).then_inc(sum_ok, 1)
                elif name == "stat3":
                    t, = a
                    stats(2, [t], x_tile, sum_ok, NTERM * (t + 1))
                elif name == "norm3":
                    norm(2, [a[0]], x_tile, xn_tile)
                elif name == "esum":
                    t, = a
                    dve.wait_ge(eprod_ok, t + 1)
                    if t >= 2:
                        dve.wait_ge(exp_ok, t - 1)
                    e2 = en[:, t % 2, :, :]
                    nc.vector.tensor_reduce(e2.rearrange("p h g -> p (h g)"),
                                            eprod[t % 2].rearrange("p (e d) -> p e d", d=DH), AX_X,
                                            ALU.add).then_inc(ered_ok, 1)
                    dve.wait_ge(ered_ok, t + 1)
                    nc.vector.tensor_reduce(mx[:, t % 2, :], e2, AX_X, ALU.max).then_inc(max_ok, 1)
                    dve.wait_ge(max_ok, t + 1)
                    nc.vector.tensor_tensor(e2, e2, mx[:, t % 2, :].unsqueeze(2).broadcast_to([P, NH, NH]),
                                            ALU.subtract).then_inc(sub_ok, 1)
                elif name == "soft":
                    t, = a
                    dve.wait_ge(exp_ok, t + 1)
                    nc.vector.tensor_reduce(sm[:, t % 2, :], pr[:, t % 2, :, :], AX_X, ALU.add).then_inc(soft_ok, 1)
                    dve.wait_ge(soft_ok, t + 1)
                    nc.vector.reciprocal(rs[:, t % 2, :], sm[:, t % 2, :]).then_inc(rs_ok, 1)
                elif name == "vsum":
                    t, = a
                    dve.wait_ge(vprod_ok, t + 1)
                    nc.vector.tensor_reduce(att[:, t % 2, :], vprod.rearrange("p (e g) -> p e g", g=NH), AX_X,
                                            ALU.add).then_inc(vred_ok, 1)
                    dve.wait_ge(vred_ok, t + 1)
                    dve.wait_ge(rs_ok, t + 1)
                    av = att[:, t % 2, :].rearrange("p (h d) -> p h d", d=DH)
                    nc.vector.tensor_tensor(av, av, rs[:, t % 2, :].unsqueeze(2).broadcast_to([P, NH, DH]),
                                            ALU.mult).then_inc(att_ok, 1)
                    stats(3, [t], lambda t: att[:, t % 2, :], att_ok, t + 1)
                elif name == "norm4":
                    norm(3, [a[0]], lambda t: att[:, t % 2, :], lambda t: on[:, t, :])
                elif name == "turn4":
                    t, = a
                    dve.wait_ge(T4_ps, t + 1)
                    if t >= 2:
                        dve.wait_ge(wo_ps, t - 1)
                    nc.vector.tensor_scalar(oT[:, t % 2, :], T4, col[:, C_LNG:C_LNG + 1], col[:, C_LNB:C_LNB + 1],
                                            ALU.mult, ALU.add).then_inc(oT_ok, 1)
                elif name == "wo":
                    t, = a
                    dve.wait_ge(wo_ps, t + 1)
                    nc.vector.scalar_tensor_tensor(x[:, t, :], WO, tg[:, G_X1:G_X1 + 1], x[:, t, :],
                                                   ALU.mult, ALU.add).then_inc(x3_ok, 1)
                    stats(4, [t], x_tile, x3_ok, t + 1)
                elif name == "norm5":
                    norm(4, [a[0]], x_tile, xn_tile)
                elif name == "lora":
                    t, = a
                    if t == 0:
                        dve.wait_ge(ld_gate, 16)
                        nc.vector.tensor_scalar(mask_s[:, :, :], mask_s[:, :, :],
                                                gate[0:NL, G_SCALE:G_SCALE + 1], None, ALU.mult).then_inc(mask_ok, 1)
                        dve.wait_ge(mask_ok, 1)
                    dve.wait_ge(fac_ps, t + 1)
                    if t >= 2:
                        dve.wait_ge(y_ps, t - 1)
                    nc.vector.tensor_copy(even1[:, t % 2, :], FAC[:, 0:P])
                    nc.vector.tensor_tensor(u_mask[:, t % 2, :, :],
                                            FAC[:, 2 * P:3 * P].unsqueeze(1).broadcast_to([NL, NL, P]),
                                            mask_s[:, :, :], ALU.mult)
                    nc.vector.tensor_tensor(
                        even2[:, t % 2, :, :, :],
                        FAC[:, P:2 * P].rearrange("p (o r) -> p r o", r=FB).unsqueeze(2).broadcast_to(
                            [NL, FB, NL, P // NL]),
                        mask_s[:, :, 0:P // NL].unsqueeze(1).broadcast_to([NL, FB, NL, P // NL]),
                        ALU.mult).then_inc(fac_ok, 1)
                elif name == "down1":
                    t, = a
                    dve.wait_ge(y_ps, t + 1)
                    nc.vector.scalar_tensor_tensor(x[:, t, :], Y5, tg[:, G_F1:G_F1 + 1], x[:, t, :],
                                                   ALU.mult, ALU.add).then_inc(y_ok, 1)

        @block.tensor
        def _(pe):
            mm = nc.tensor.matmul

            def bank_free(*item):
                n = WORK.index(item) - NWORK
                if n < 0:
                    return
                kind, *b = WORK[n]
                if kind == "kv":
                    pe.wait_ge(kv_ok, b[0] + 1)
                elif kind == "up":
                    pe.wait_ge(up_ok, NTH_UP[b[0], b[1]] * FB + b[2] + 1)
                else:
                    pe.wait_ge(sum_ok, (b[0] + 1) * CHUNK)

            def project(dst, lhsT, w0, r0, n):
                mm(dst, lhsT, sw[:, w0:w0 + n], start=True, stop=False)
                return mm(dst, ones_row[:, :], row[:, r0:r0 + n], start=False, stop=True)

            for name, *a in TIMELINE:
                if name == "kv":
                    if a[0] == 0:
                        pe.wait_ge(ld_ctx, 16)
                        pe.wait_ge(ld_small, 16)
                        pe.wait_ge(ld_row, 16)
                        pe.wait_ge(consts, 1)
                    for t in range(a[0] * GT, a[0] * GT + GT):
                        bank_free("kv", t)
                        project(work_bank("kv", t)[:, 0:2 * D], ctxT_sb[:, t * P:(t + 1) * P], S_KV, R_KV, 2 * D).then_inc(kv_ps, 1)
                elif name == "mix":
                    g, = a
                    pe.wait_ge(scan_ok, g + 1)
                    pe.wait_ge(diag_ok, 1)
                    if g:
                        pe.wait_ge(mixed_ok, g)
                    for s, dst in ((1, ps_den), (0, ps_num)):
                        for i in range(GT):
                            o = (g * GT + i) * SEG
                            d = dst[:, i * D:(i + 1) * D]
                            mm(d, fwd[:, s, o:o + P], ident[:, :], start=True, stop=False)
                            mm(d, bwd[:, s, o + 2:o + 2 + P], ident[:, :], start=False, stop=False)
                            last = mm(d, src[:, s, o + 1:o + 1 + P], diag_u[:, :], start=False, stop=True)
                    last.then_inc(mix_ps, 1)
                elif name == "rows":
                    g, = a
                    pe.wait_ge(norm_ok[1], g + 1)
                    if g:
                        pe.wait_ge(xnT_ok, g)
                    for i in range(GT):
                        last = nc.tensor.transpose(ps_turn[:, i * P:(i + 1) * P], xn[:, g * GT + i, :], ident[:, :])
                    last.then_inc(turn_ps, 1)
                    pe.wait_ge(xnT_ok, g + 1)
                    for t in range(g * GT, g * GT + GT):
                        last = mm(ps_logit[:, t * NE:(t + 1) * NE], xnT[:, t, :], sw[:, S_R:S_R + NE],
                                  start=True, stop=True)
                    last.then_inc(logit_ps, 1)
                elif name == "rank":
                    e, = a
                    d = ps_rank[:, e * NB:(e + 1) * NB]
                    pe.wait_ge(elig_ok, 2 * e + 2)
                    mm(d, tri[:, :], elig[:, e, :], start=True, stop=False)
                    mm(d, ones_bf[:, :], before[:, e, 0:NB], start=False, stop=True).then_inc(rank_ps, 1)
                elif name == "coef":
                    pe.wait_ge(coef_ok, 1)
                    for g in range(NG):
                        pe.wait_ge(coefT_ok, g) if g else pe.wait_ge(xnT_ok, NG)
                        for i in range(GT):
                            last = nc.tensor.transpose(ps_turn[0:NF, i * P:(i + 1) * P], coef[:, g * GT + i, :],
                                                       ident[:, :])
                        last.then_inc(coefT_ps, 1)
                elif name == "up":
                    g, e, j = a
                    if j == 0:
                        pe.wait_ge(ld_up[e], 16)
                        pe.wait_ge(xnT_ok, g + 1)
                    bank_free("up", g, e, j)
                    mm(work_bank("up", g, e, j)[:, :], wu[:, e, j * P:(j + 1) * P],
                       xnT[:, g * GT:(g + 1) * GT, :].rearrange("p b t -> p (b t)"),
                       start=True, stop=True).then_inc(up_ps, 1)
                elif name == "down":
                    c, = a
                    bank_free("down", c)
                    for n in range(c * CHUNK, (c + 1) * CHUNK):
                        t, e = TERMS[n]
                        if e is None:
                            pe.wait_ge(ld_b2, 16)
                            pe.wait_ge(coefT_ok, NG)
                            last = mm(place(n), coefT[:, t, :], b2_sb[:, :], start=True, stop=True)
                            continue
                        pe.wait_ge(ld_dn[e], 16)
                        pe.wait_ge(up_ok, (NTH_UP[t // GT, e] + 1) * FB)
                        for j in range(FB):
                            last = mm(place(n), hid[:, e, j, t % GT * P:(t % GT + 1) * P], wd[:, e, j, :],
                                      start=(j == 0), stop=(j == FB - 1))
                    last.then_inc(down_ps, 1)
                elif name == "turn3":
                    t, = a
                    pe.wait_ge(norm_ok[2], t + 1)
                    if t:
                        pe.wait_ge(q_ok, t)
                    nc.tensor.transpose(T3, xn[:, t, :], ident[:, :]).then_inc(T3_ps, 1)
                elif name == "query":
                    t, = a
                    pe.wait_ge(T3_ok, t + 1)
                    project(Q, xT3[:, t % 2, :], S_Q, R_Q, D).then_inc(q_ps, 1)
                elif name == "turn4":
                    t, = a
                    pe.wait_ge(norm_ok[3], t + 1)
                    if t:
                        pe.wait_ge(x3_ok, t)
                    nc.tensor.transpose(T4, on[:, t, :], ident[:, :]).then_inc(T4_ps, 1)
                elif name == "wo":
                    t, = a
                    pe.wait_ge(oT_ok, t + 1)
                    project(WO, oT[:, t % 2, :], S_O, R_O, D).then_inc(wo_ps, 1)
                elif name == "turn5":
                    t, = a
                    pe.wait_ge(norm_ok[4], t + 1)
                    if t:
                        pe.wait_ge(fac_ok, t)
                    nc.tensor.transpose(T5, xn[:, t, :], ident[:, :]).then_inc(T5_ps, 1)
                elif name == "lora":
                    t, = a
                    pe.wait_ge(T5_ok, t + 1)
                    mm(FAC[:, 0:P], ident[:, 1:1 + 2 * NL:2], xn[:, t, :], start=True, stop=True)
                    mm(FAC[:, P:2 * P], ident[:, 1 + 2 * NL:1 + 4 * NL:2], xn[:, t, :], start=True, stop=True)
                    mm(FAC[:, 2 * P:3 * P], xT5[:, t % 2, 2:2 + 2 * NL:2], xT5[:, t % 2, :],
                       start=True, stop=True).then_inc(fac_ps, 1)
                elif name == "up1":
                    t, = a
                    pe.wait_ge(fac_ok, t + 1)
                    pe.wait_ge(ld_l1, 32)
                    if t:
                        pe.wait_ge(low_ok, t)
                    for j in range(FB):
                        d = ps_h1[:, j * P:(j + 1) * P]
                        mm(d, w1u[:, j * P:(j + 1) * P], xT5[:, t % 2, :], start=True, stop=False)
                        last = mm(d, even1[:, t % 2, :], u_mask[:, t % 2, j, :], start=False, stop=True)
                    last.then_inc(up1_ps, 1)
                elif name == "low2":
                    t, = a
                    pe.wait_ge(hid1_ok, t + 1)
                    mm(ps_h1[0:NL, :], xT5[:, t % 2, 2 + 2 * NL:2 + 4 * NL:2],
                       hid1[:, t % 2, :, :].rearrange("p r t -> p (r t)"), start=True, stop=True).then_inc(low_ps, 1)
                elif name == "down1":
                    t, = a
                    pe.wait_ge(low_ok, t + 1)
                    if t:
                        pe.wait_ge(y_ok, t)
                    for r in range(FB):
                        mm(Y5, hid1[:, t % 2, r, :], w1d[:, r, :], start=(r == 0), stop=False)
                    for r in range(FB):
                        mm(Y5, low[:, t % 2, r, :], even2[:, t % 2, r, :, :].rearrange("p j o -> p (j o)"),
                           start=False, stop=False)
                    mm(Y5, ones_row[:, :], row[:, R_B2:R_B2 + D], start=False, stop=True).then_inc(y_ps, 1)


def kernel(**inputs):
    import numpy as np
    import concourse.bacc as bacc
    from concourse.bass_utils import run_bass_kernel_spmd

    a = {k: np.asarray(v) for k, v in inputs.items()}

    def hidden_cols(b):
        return b.reshape(-1, P).T

    w_up = np.concatenate([a["L0_ffn_W1"], a["L0_ffn_fw1"][None]]).transpose(1, 0, 2)
    w_down = np.concatenate([a["L0_ffn_W2"], a["L0_ffn_fw2"][None]]).reshape(NF, FB, P, D).transpose(2, 0, 1, 3)
    by_dim = a["L1_xattn_Wv"].reshape(NH, DH, D).transpose(1, 0, 2).reshape(D, D)
    arrays = {
        "ctxT": a["ctx_1024"].transpose(2, 0, 1).reshape(D, NB * P),
        "x_in": a["x"].transpose(1, 0, 2).reshape(P, NB * D),
        "cols": np.concatenate([a["L0_xattn_w"].reshape(D, 1), a["L0_xattn_u"].reshape(D, 1),
                                a["L1_xattn_ln_g"].reshape(D, 1), a["L1_xattn_ln_b"].reshape(D, 1),
                                hidden_cols(a["L0_ffn_b1"]), hidden_cols(a["L0_ffn_fb1"]),
                                hidden_cols(a["L1_ffn_b1"])], axis=1),
        "gates": np.stack([a["g_xattn"][0], a["g_ffn"][0], a["g_xattn"][1], a["g_ffn"][1],
                           a["L1_ffn_scale"]]).reshape(1, 5),
        "rows": np.concatenate([a["L1_xattn_bk"], a["L1_xattn_bv"].reshape(NH, DH).T.reshape(D), a["L1_xattn_bq"],
                                a["L1_xattn_bo"], a["L1_ffn_b2"]]).reshape(1, NROW),
        "small": np.concatenate([a["L1_xattn_Wk"].T, by_dim.T, a["L1_xattn_Wq"].T, a["L1_xattn_Wo"].T,
                                 a["L0_ffn_Wr"]], axis=1),
        "w_up": w_up,
        "w_down": w_down,
        "b2": np.concatenate([a["L0_ffn_b2"], a["L0_ffn_fb2"][None]]),
        "l1_up": a["L1_ffn_W1"].T,
        "l1_down": a["L1_ffn_W2"].T.reshape(FB, P, D).transpose(1, 0, 2),
    }
    arrays = {k: np.ascontiguousarray(v) for k, v in arrays.items()}
    nc = bacc.Bacc("TRN2", target_bir_lowering=False, num_devices=1)
    aps = [nc.dram_tensor(k, v.shape, mybir.dt.from_np(v.dtype), kind="ExternalInput").ap()
           for k, v in arrays.items()]
    out = nc.dram_tensor("out", (NB, P, D), F32, kind="ExternalOutput").ap()
    flamingo_kernel(nc, *aps, out)
    r = run_bass_kernel_spmd(nc, [arrays], core_ids=[0])
    return r.results[0]["out"]
```

```python
from contextlib import ExitStack

import concourse.bass as bass
from concourse import mybir

P = 128
NB = 8
GT = 2
NG = NB // GT
D = 128
FF = 512
FB = FF // P
NE = 8
FALL = NE
NF = NE + 1
CAP = max(int(1.25 * (4 * 256 * 2 / NE)), 4)
NH = 16
DH = D // NH
NL = 4
EPS = 1e-5
SEG = P + 1
SCAN = NB * SEG + 1
NTERM = NF + 1
CHUNK = 2
PAIRS = FB // 2
HG = 5
S_X, S_WT = 16.0, 256.0
NSTAGE = 5
NWORK = 3
INV_SQRT_D = float(D) ** -0.5

ALU = mybir.AluOpType
ACT = mybir.ActivationFunctionType
F32 = mybir.dt.float32
BF16 = mybir.dt.bfloat16
F16 = mybir.dt.float16
U32 = mybir.dt.uint32
AX_X = mybir.AxisListType.X

C_W, C_U, C_LNG, C_LNB, C_B1 = 0, 1, 2, 3, 4
C_L1B1 = C_B1 + NF * FB
NCOL = C_L1B1 + FB
S_KV, S_Q, S_O, S_R = 0, 2 * D, 3 * D, 4 * D
NSMALL = 4 * D + NE
R_KV, R_Q, R_O, R_B2 = 0, 2 * D, 3 * D, 4 * D
NROW = 5 * D
G_X0, G_F0, G_X1, G_F1, G_SCALE = range(5)

PIECES = {
    "stat3": (-0.78, -1.23, -1.23, -1.23), "norm3": (1.48, 1.48, 1.48, 1.48), "turn3": (2.5, 2.5, 2.5, 5.29),
    "query": (3.5, 3.5, 3.5, 3.5), "eprod": (4.5, 4.5, 4.5, 4.5), "esum": (7, 7, 7.7, 7), "vprod": (11, 11, 11, 11),
    "soft": (13.41, 13.41, 8.14, 13.41), "vsum": (14, 14, 14, 14), "norm4": (18, 18, 18, 18),
    "turn4": (19.39, 18.5, 18.5, 18.5), "wo": (20, 20, 20, 20), "stat5": (21, 21.41, 21, 21),
    "norm5": (26.63, 26.63, 26.63, 26.63), "turn5": (27.13, 27.13, 27.13, 27.13),
    "lora": (29.32, 29.32, 29.32, 29.32), "up1": (32.87, 32.87, 32.87, 32.87), "low2": (37.17, 37.17, 37.17, 37.17),
    "down1": (43.34, 44.02, 43.34, 43.34),
}
START = {
    ("split", FALL): (-20, -20, -20, -20), ("split", 0): (-19, -19, -19, -17), ("split", 1): (-17, -17, -17, -15),
    ("split", 2): (-15, -15, -15, -14), ("split", 3): (-13.5, -15, -13.5, -12.5), ("split", 4): (-12, -15, -12, -11),
    ("split", 5): (-10.5, -15, -10.5, -9.5), ("split", 6): (-9, -15, -9, -8), ("split", 7): (-7.5, -15, -7.5, -6.5),
    ("mix", 0): (-23.77, -19.77, -19.77, -19.77), ("stat1", 0): (-19, -19, -19, -19),
    ("scan", 2): (-16, -18, -16, -16), ("rows", 0): (-15, -17.5, -17.5, -15), ("xlow", 0): (-15, -16, -15, -15),
    ("logits", 0): (-0.74, -9.74, -9.74, -9.74), ("mix", 1): (-18, -17, -18, -18), ("stat1", 1): (-12, -15, -12, -16),
    ("scan", 3): (-11, -14, -11, -11), ("rows", 1): (-3, -13, -13, -1), ("xlow", 1): (0, -11, 0, 0),
    ("logits", 1): (0, 4, 4, 4), ("mix", 2): (-9, -12, -9, -9), ("stat1", 2): (-8, -10, -8, -12),
    ("rows", 2): (2, -8, 2, 1), ("xlow", 2): (0, -6, 0, 0), ("logits", 2): (5, 9, 9, 9),
    ("mix", 3): (-0.54, -7, -5, -5), ("stat1", 3): (2, -6.5, -4, -8), ("rows", 3): (7, -4, 7, 12),
    ("xlow", 3): (0, -2, 0, 0), ("logits", 3): (9, 13, 13, 13), ("kv", 0): (-2.5, -4.8, -2.5, -1),
    ("kv", 1): (2, 2, 2, 2), ("kv", 2): (7, 7, 7, 7), ("kv", 3): (18.59, 18.59, 18.59, 18.59),
    ("choose",): (14, -1, 11, 14), ("choose2",): (15, 0, 11, 15), ("rank", 0): (11, 1, 1, 1),
    ("rank", 1): (12.3, 2, 1, 1), ("rank", 2): (13.6, 3, 1, 1), ("rank", 3): (14.9, 4, 1, 1),
    ("rank", 4): (16.2, 5, 1, 1), ("rank", 5): (17.5, 6, 1, 1), ("rank", 6): (18.8, 7, 1, 1),
    ("rank", 7): (20.1, 8, 1, 1), ("coef",): (22.26, 8.76, 22.26, 22.26),
}
T_UP, T_DOWN = 0.640, 1.733
T_COEF = 26.00
FFNS = (FALL, *range(NE))


def timeline(engine):
    items = []
    at = 0.0

    def put(when, *item):
        items.append((when, len(items), item))

    def up(g, ffns):
        nonlocal at
        for e in ffns:
            for i in range(PAIRS):
                put(at, "up", g, e, i)
                at += T_UP

    def down(c):
        nonlocal at
        put(at, "down", c)
        at += T_DOWN
        t, last = divmod(c + 1, NTERM // CHUNK)
        if last == 0:
            for piece, lags in PIECES.items():
                put(at + lags[engine], piece, t - 1)

    for item, lags in START.items():
        put(lags[engine], *item)
    up(0, FFNS)
    up(1, FFNS)
    at = max(at, T_COEF)
    per_tile = NTERM // CHUNK
    for g in range(NG):
        for c in range(per_tile):
            down(2 * g * per_tile + c)
        for c in range(per_tile):
            down((2 * g + 1) * per_tile + c)
            if g + 2 < NG:
                up(g + 2, [e for _, e in TERMS[c * CHUNK:(c + 1) * CHUNK] if e is not None])
    return [item for _, _, item in sorted(items, key=lambda x: x[:2])]


NTH_UP = {(g, e): g * NF + i for g in range(NG) for i, e in enumerate(FFNS)}
TERMS = [(t, e) for t in range(NB) for e in (None, *FFNS)]
PE_ORDER, DVE_ORDER, ACT_ORDER, POOL_ORDER = (timeline(i) for i in range(4))
WORK = [("kv", t) if item[0] == "kv" else item for item in PE_ORDER if item[0] in ("kv", "up", "down")
        for t in (range(item[1] * GT, item[1] * GT + GT) if item[0] == "kv" else (0,))]


def flamingo_kernel(nc, ctxT, x_in, cols, gates, rows, small, w_up, w_down, b2, l1_up, l1_down, out):
    with ExitStack() as ctx:
        def sb(name, shape, dt=F32):
            return ctx.enter_context(nc.sbuf_tensor(name, shape, dt))

        def bank(name):
            return ctx.enter_context(nc.psum_tensor(name, [P, 512], F32))

        def sem(name):
            return ctx.enter_context(nc.semaphore(name))

        ctxT_sb = sb("ctxT_sb", [P, NB * P])
        x = sb("x", [P, NB, D])
        xn = sb("xn", [P, NB, D])
        col = sb("col", [P, NCOL])
        gate = sb("gate", [P, 5])
        tg = sb("tg", [P, 4])
        row5 = sb("row5", [NROW // D, D])
        row_part = sb("row_part", [NROW // D, 3, D], BF16)
        row3 = sb("row3", [3, NROW], BF16)
        sw = sb("sw", [P, NSMALL])
        w_stage = sb("w_stage", [P, NSTAGE, FF])
        wu = sb("wu", [P, 2, NF, FF], F16)
        wr = sb("wr", [P, 2, NE], F16)
        wd = sb("wd", [P, NF, FB, D])
        b2_sb = sb("b2_sb", [NF, D])
        w1u = sb("w1u", [P, FF])
        w1d = sb("w1d", [P, FB, D])
        ew = sb("ew", [P, 2])
        decay = sb("decay", [P, SCAN])
        src = sb("src", [P, 2, SCAN])
        fwd = sb("fwd", [P, 2, SCAN])
        bwd = sb("bwd", [P, 2, SCAN])
        diag_u = sb("diag_u", [P, P])
        ident = sb("ident", [P, P])
        tri = sb("tri", [P, P], BF16)
        ones_bf = sb("ones_bf", [P, P], BF16)
        ones3 = sb("ones3", [3, P], BF16)
        iota_e = sb("iota_e", [P, NE])
        minus_half = sb("minus_half", [P, NB])
        one8 = sb("one8", [P, NB])
        mask_s = sb("mask_s", [NL, NL, P])
        mask16 = sb("mask16", [FB * NL, NL, P // NL])
        pick = sb("pick", [P, FB, FB * NL])
        on = sb("on", [P, NB, D])
        mixed = sb("mixed", [P, 2, GT * D])
        bn = sb("bn", [P, NB, 6])
        mv = sb("mv", [P, 5, NB, 2])
        ve = sb("ve", [P, 5, NB])
        rstd = sb("rstd", [P, 5, NB])
        neg_rstd = sb("neg_rstd", [P, NB])
        mu_rstd = sb("mu_rstd", [P, NB])
        xnT = sb("xnT", [P, 2, NB, P], F16)
        hid = sb("hid", [P, 2, NF, FB, GT * P])
        k_sb = sb("k_sb", [P, NB, D])
        v_sb = sb("v_sb", [P, NB, D])
        logit = sb("logit", [P, NB, NE])
        top = sb("top", [P, NB, 8])
        topi = sb("topi", [P, NB, 8], U32)
        topf = sb("topf", [P, NB, 2])
        gap = sb("gap", [P, NB])
        egap = sb("egap", [P, NB])
        den2 = sb("den2", [P, NB])
        wt = sb("wt", [P, 2, NB])
        hot = sb("hot", [P, 2, NB, NE])
        assign = sb("assign", [P, NB, NE])
        weight = sb("weight", [P, NB, NE])
        live = sb("live", [P, NB])
        over = sb("over", [P, NB])
        elig = sb("elig", [P, NE, NB], BF16)
        before = sb("before", [P, NE, NB + 1], BF16)
        coef = sb("coef", [P, NB, NF])
        coefT = sb("coefT", [NF, NB, P])
        q_sb = sb("q_sb", [P, 2, D])
        xT3 = sb("xT3", [P, 2, P])
        oT = sb("oT", [P, 2, P])
        xT5 = sb("xT5", [P, 2, P])
        en = sb("en", [P, 2, NH, NH])
        mx = sb("mx", [P, 2, NH])
        pr = sb("pr", [P, 2, NH, NH])
        sm = sb("sm", [P, 2, NH])
        rs = sb("rs", [P, 2, NH])
        att = sb("att", [P, 2, D])
        odd2 = sb("odd2", [P, 2, FB * (FB * NL + NL)])

        eprod = [fwd[:, :, :].rearrange("p a s -> p (a s)")[:, 0:NH * NH * DH],
                 bwd[:, :, :].rearrange("p a s -> p (a s)")[:, 0:NH * NH * DH]]
        vprod = src[:, :, :].rearrange("p a s -> p (a s)")[:, 0:NH * NH * DH]
        u_mask = decay[0:NL, 0:2 * NL * P].rearrange("p (i j t) -> p i j t", i=2, j=NL)
        hid1 = ctxT_sb[:, :].rearrange("p (i r t) -> p i r t", i=2, r=FB)

        even1 = w_stage[0:NL, 0, 0:2 * P].rearrange("p (i t) -> p i t", i=2)
        low = w_stage[0:FB * NL, 1, 0:2 * P].rearrange("p (i t) -> p i t", i=2)
        even2 = w_stage[0:FB * NL, 2, 0:2 * P].rearrange("p (i j o) -> p i j o", i=2, j=NL)

        work = [bank(f"ps_work{i}") for i in range(NWORK)]
        ps_num = bank("ps_num")
        ps_den = bank("ps_den")
        ps_turn = bank("ps_turn")
        ps_logit = bank("ps_logit")
        ps_rank = bank("ps_rank")
        ps_q, ps_o, ps_x5, ps_h1, ps_y = ps_num, ps_den, ps_turn, ps_logit, ps_rank
        T3, Q = ps_q[:, 0:P], ps_q[:, P:2 * P]
        T4, WO = ps_o[:, 0:P], ps_o[:, P:2 * P]
        T5, EVEN1, U1, EVEN2 = ps_x5[:, 0:P], ps_x5[0:NL, P:2 * P], ps_x5[0:NL, 2 * P:3 * P], \
            ps_x5[0:FB * NL, 3 * P:3 * P + P // NL]
        Y5 = ps_y[:, 0:D]

        def work_bank(*item):
            return work[WORK.index(item) % NWORK]

        def place(n):
            return work_bank("down", n // CHUNK)[:, n % CHUNK * D:(n % CHUNK + 1) * D]

        def seg(buf, a, g, off):
            v = buf[:, a, off:off + NB * SEG] if off + NB * SEG <= SCAN else None
            return v.rearrange("p (b s) -> p b s", s=SEG)[:, g * GT:(g + 1) * GT, 0:P]

        ld_ctx, ld_x, ld_col, ld_gate, ld_row, ld_small, ld_b2, ld_l1 = (
            sem(f"ld_{n}") for n in ("ctx", "x", "col", "gate", "row", "small", "b2", "l1"))
        ld_up = [sem(f"ld_up{e}") for e in range(NF)]
        ld_dn = [sem(f"ld_dn{e}") for e in range(NF)]
        consts, zeroed, masks, mask_ok = sem("consts"), sem("zeroed"), sem("masks"), sem("mask_ok")
        row_step, row3_ok, scaled, high_ok, split_ok, xhigh_ok, odd2_ok = (
            sem(n) for n in ("row_step", "row3_ok", "scaled", "high_ok", "split_ok", "xhigh_ok", "odd2_ok"))
        mask16_step = sem("mask16_step")
        wr_step, eprod2_ok, vprod2_ok = sem("wr_step"), sem("eprod2_ok"), sem("vprod2_ok")
        ew_ok, tg_ok, ek_ok, decay_ok, diag_ok = (sem(n) for n in ("ew_ok", "tg_ok", "ek_ok", "decay_ok", "diag_ok"))
        ekv_ok, scan_ok = sem("ekv_ok"), sem("scan_ok")
        kv_ps, kv_ok = sem("kv_ps"), sem("kv_ok")
        bn_ok, aggr_ok, ve_ok, rstd_ok, norm_ok = ([sem(f"{n}{i}") for i in range(5)] for n in (
            "bn_ok", "aggr_ok", "ve_ok", "rstd_ok", "norm_ok"))
        er_ok, mix_ps, dn_ok, rec_ok, mixed_ok, x1_ok = (
            sem(n) for n in ("er_ok", "mix_ps", "dn_ok", "rec_ok", "mixed_ok", "x1_ok"))
        turn_ps, xnT_ok, logit_ps, logit_ok = (sem(n) for n in ("turn_ps", "xnT_ok", "logit_ps", "logit_ok"))
        ch, egap_ok = sem("choose_step"), sem("egap_ok")
        rk, elig_ok, rank_ps = sem("rank_step"), sem("elig_ok"), sem("rank_ps")
        coef_ok, coefT_ps, coefT_ok = (
            sem(n) for n in ("coef_ok", "coefT_ps", "coefT_ok"))
        up_ps, up_ok, down_ps, sum_ok = (sem(n) for n in ("up_ps", "up_ok", "down_ps", "sum_ok"))
        T3_ps, T3_ok, q_ps, q_ok = (sem(n) for n in ("T3_ps", "T3_ok", "q_ps", "q_ok"))
        eprod_ok, ered_ok, max_ok, sub_ok, exp_ok, vprod_ok, soft_ok, rs_ok, vred_ok, att_ok = (
            sem(n) for n in ("eprod_ok", "ered_ok", "max_ok", "sub_ok", "exp_ok", "vprod_ok", "soft_ok", "rs_ok",
                             "vred_ok", "att_ok"))
        T4_ps, oT_ok, wo_ps, x3_ok, T5_ps, T5_ok = (
            sem(n) for n in ("T4_ps", "oT_ok", "wo_ps", "x3_ok", "T5_ps", "T5_ok"))
        fac_ps, fac_ok, up1_ps, hid1_ok, low_ps, low_ok, y_ps, y_ok, stored = (
            sem(n) for n in ("fac_ps", "fac_ok", "up1_ps", "hid1_ok", "low_ps", "low_ok", "y_ps", "y_ok", "stored"))

        def query_key_products(ops, eng, t, h0, h1, done):
            eng.wait_ge(q_ok, t + 1)
            eng.wait_ge(kv_ok, t + 1)
            if t >= 2:
                eng.wait_ge(ered_ok, t - 1)
            shape = [P, h1 - h0, NH, DH]
            qv = q_sb[:, t % 2, h0 * DH:h1 * DH].rearrange("p (h g d) -> p h g d", h=h1 - h0, g=1).broadcast_to(shape)
            kv = k_sb[:, t, :].rearrange("p (h g d) -> p h g d", h=1, g=NH).broadcast_to(shape)
            ops.tensor_tensor(eprod[t % 2].rearrange("p (h g d) -> p h g d", h=NH, g=NH)[:, h0:h1, :, :], qv, kv,
                              ALU.mult).then_inc(done, 1)

        def weight_value_products(ops, eng, t, h0, h1, done):
            eng.wait_ge(exp_ok, t + 1)
            if t >= 1:
                eng.wait_ge(vred_ok, t)
            shape = [P, h1 - h0, DH, NH]
            pv = pr[:, t % 2, h0:h1, :].unsqueeze(2).broadcast_to(shape)
            vv = v_sb[:, t, :].rearrange("p (h d g) -> p h d g", h=1, g=NH).broadcast_to(shape)
            ops.tensor_tensor(vprod.rearrange("p (h d g) -> p h d g", h=NH, d=DH)[:, h0:h1, :, :], pv, vv,
                              ALU.mult).then_inc(done, 1)

        block = ctx.enter_context(nc.Block())

        @block.sync
        def _(sp):
            sp.dma_start(ctxT_sb[:, :], ctxT).then_inc(ld_ctx, 16)
            sp.dma_start(col[:, :], cols).then_inc(ld_col, 16)
            sp.dma_start(x[:, :, :].rearrange("p b d -> p (b d)"), x_in).then_inc(ld_x, 16)
            sp.dma_start(sw[:, :], small).then_inc(ld_small, 16)
            sp.dma_start(row5[:, :], rows).then_inc(ld_row, 16)
            sp.dma_start(gate[:, :], gates.broadcast_to([P, 5])).then_inc(ld_gate, 16)
            for n, e in enumerate(FFNS[:NSTAGE]):
                sp.dma_start(w_stage[:, n, :], w_up[:, e, :]).then_inc(ld_up[e], 16)
            for n, e in enumerate(FFNS[NSTAGE:], NSTAGE):
                sp.wait_ge(split_ok, n - NSTAGE + 1)
                sp.dma_start(w_stage[:, n % NSTAGE, :], w_up[:, e, :]).then_inc(ld_up[e], 16)
            sp.wait_ge(row_step, 5)
            for i in range(3):
                sp.dma_start(row3[i:i + 1, :], row_part[:, i, :]).then_inc(row3_ok, 16)
            for e in FFNS:
                sp.dma_start(wd[:, e, :, :], w_down[:, e, :, :]).then_inc(ld_dn[e], 16)
            sp.dma_start(b2_sb[:, :], b2).then_inc(ld_b2, 16)
            sp.dma_start(w1u[:, :], l1_up).then_inc(ld_l1, 16)
            sp.dma_start(w1d[:, :, :], l1_down).then_inc(ld_l1, 16)
            for t in range(NB):
                sp.wait_ge(y_ok, t + 1)
                sp.dma_start(out[t, :, :], x[:, t, :]).then_inc(stored, 16)
            sp.wait_ge(stored, 16 * NB)

        @block.gpsimd
        def _(pool):
            nc.gpsimd.memset(ident[:, :], 0.0).then_inc(zeroed, 1)
            nc.gpsimd.memset(decay[:, :], 1.0).then_inc(zeroed, 1)
            nc.gpsimd.memset(ones3[:, :], 1.0)
            nc.gpsimd.memset(pick[:, :, :], 0.0)
            nc.gpsimd.memset(odd2[:, :, :], 0.0)
            nc.gpsimd.memset(mask16[:, :, :], 0.0)
            nc.gpsimd.memset(minus_half[:, :], -0.5)
            nc.gpsimd.memset(one8[:, :], 1.0)
            nc.gpsimd.memset(ones_bf[:, :], 1.0).then_inc(zeroed, 1)
            nc.gpsimd.memset(mask_s[:, :, :], 0.0).then_inc(zeroed, 1)
            pool.wait_ge(zeroed, 4)
            nc.gpsimd.affine_select(out=ident[:, :], in_=ident[:, :], compare_op=ALU.not_equal, fill=1.0, base=0,
                                    pattern=[[-1, P]], channel_multiplier=1)
            nc.gpsimd.affine_select(out=tri[:, :], in_=ones_bf[:, :], compare_op=ALU.is_ge, fill=0.0, base=0,
                                    pattern=[[1, P]], channel_multiplier=-1)
            nc.gpsimd.affine_select(out=mask_s[:, :, :], in_=mask_s[:, :, :], compare_op=ALU.not_equal, fill=1.0,
                                    base=0, pattern=[[-1, NL], [0, P]], channel_multiplier=1)
            for r in range(FB):
                nc.gpsimd.affine_select(out=mask16[:, :, :], in_=mask16[:, :, :], compare_op=ALU.not_equal, fill=1.0,
                                        base=-NL * r, pattern=[[-1, NL], [0, P // NL]],
                                        channel_multiplier=1).then_inc(mask16_step, 1)
                pool.wait_ge(mask16_step, r + 1)
            nc.gpsimd.iota(iota_e[:, :], [[1, NE]], base=0, channel_multiplier=0,
                           allow_small_or_imprecise_dtypes=True).then_inc(consts, 1)
            pool.wait_ge(consts, 1)
            for r in range(FB):
                last = nc.gpsimd.tensor_copy(pick[:, r, NL * r:NL * (r + 1)],
                                             ident[:, 1 + 2 * NL:1 + 4 * NL:2])
            last.then_inc(consts, 1)

            def root(i, a, b, count):
                pool.wait_ge(ve_ok[i], count)
                nc.gpsimd.tensor_tensor(rstd[:, i, a:b], ve[:, i, a:b], minus_half[:, 0:b - a],
                                        ALU.pow).then_inc(rstd_ok[i], 1)

            pool.wait_ge(ew_ok, 1)
            nc.gpsimd.tensor_scalar(diag_u[:, :], ident[:, :], ew[:, 1:2], None, ALU.mult).then_inc(diag_ok, 1)
            root(0, 0, NB, 1)
            pool.wait_ge(ld_row, 16)
            for i in range(3):
                nc.gpsimd.tensor_copy(row_part[:, i, :], row5[:, :]).then_inc(row_step, 1)
                if i < 2:
                    pool.wait_ge(row_step, 2 * i + 1)
                    nc.gpsimd.tensor_tensor(row5[:, :], row5[:, :], row_part[:, i, :],
                                            ALU.subtract).then_inc(row_step, 1)
                    pool.wait_ge(row_step, 2 * i + 2)
            for name, *a in POOL_ORDER:
                if name == "split":
                    n = FFNS.index(a[0])
                    pool.wait_ge(high_ok, n + 1)
                    pool.wait_ge(scaled, n + 1)
                    nc.gpsimd.tensor_tensor(wu[:, 1, a[0], :], w_stage[:, n % NSTAGE, :], wu[:, 0, a[0], :],
                                            ALU.subtract).then_inc(split_ok, 1)
                elif name == "stat1":
                    root(1, GT * a[0], GT * a[0] + GT, a[0] + 1)
                elif name == "stat3":
                    root(2, a[0], a[0] + 1, a[0] + 1)
                elif name == "vsum":
                    root(3, a[0], a[0] + 1, a[0] + 1)
                elif name == "stat5":
                    root(4, a[0], a[0] + 1, a[0] + 1)
                elif name == "eprod":
                    query_key_products(nc.gpsimd, pool, a[0], 0, HG, eprod_ok)
                elif name == "vprod":
                    weight_value_products(nc.gpsimd, pool, a[0], 0, HG, vprod_ok)

        @block.scalar
        def _(act):
            act.wait_ge(ld_col, 16)
            nc.scalar.activation(ew[:, :], col[:, C_W:C_U + 1], ACT.Exp).then_inc(ew_ok, 1)
            act.wait_ge(ld_ctx, 16)
            for g in range(NG):
                nc.scalar.activation(seg(src, 1, g, 1),
                                     ctxT_sb[:, :].rearrange("p (b s) -> p b s", s=P)[:, g * GT:(g + 1) * GT, :],
                                     ACT.Exp).then_inc(ek_ok, 1)
            act.wait_ge(ld_small, 16)
            nc.scalar.activation(wr[:, 0, :], sw[:, S_R:S_R + NE], ACT.Copy, scale=S_WT).then_inc(wr_step, 1)
            act.wait_ge(ld_gate, 16)
            nc.scalar.activation(tg[:, :], gate[:, 0:4], ACT.Tanh).then_inc(tg_ok, 1)
            act.wait_ge(norm_ok[0], 1)
            for t in range(NB):
                nc.scalar.activation(on[:, t, :], x[:, t, :], ACT.Exp, scale=neg_rstd[:, t:t + 1],
                                     bias=mu_rstd[:, t:t + 1]).then_inc(er_ok, 1)
            for name, *a in ACT_ORDER:
                if name == "split":
                    act.wait_ge(ld_up[a[0]], 16)
                    w = w_stage[:, FFNS.index(a[0]) % NSTAGE, :]
                    nc.scalar.activation(wu[:, 0, a[0], :], w, ACT.Copy, scale=S_WT).then_inc(high_ok, 1)
                    nc.scalar.activation(w, w, ACT.Copy, scale=S_WT).then_inc(scaled, 1)
                elif name == "kv":
                    for t in range(a[0] * GT, a[0] * GT + GT):
                        act.wait_ge(kv_ps, t + 1)
                        nc.scalar.copy(k_sb[:, t, :], work_bank("kv", t)[:, 0:D])
                        nc.scalar.copy(v_sb[:, t, :], work_bank("kv", t)[:, D:2 * D]).then_inc(kv_ok, 1)
                elif name == "rows":
                    g, = a
                    act.wait_ge(turn_ps, g + 1)
                    nc.scalar.activation(xnT[:, 0, g * GT:(g + 1) * GT, :].rearrange("p b t -> p (b t)"),
                                         ps_turn[:, 0:GT * P], ACT.Copy, scale=S_X).then_inc(xhigh_ok, 1)
                elif name == "choose2":
                    act.wait_ge(ch, 3)
                    nc.scalar.activation(egap[:, :], gap[:, :], ACT.Exp).then_inc(egap_ok, 1)
                elif name == "up":
                    g, e, i = a
                    n = NTH_UP[g, e] * PAIRS + i
                    act.wait_ge(up_ps, n + 1)
                    if g >= 2:
                        act.wait_ge(down_ps, TERMS.index((g * GT - GT - 1, e)) // CHUNK + 1)
                    for k in range(2):
                        j = 2 * i + k
                        last = nc.scalar.activation(hid[:, g % 2, e, j, :],
                                                    work_bank("up", g, e, i)[:, k * GT * P:(k + 1) * GT * P],
                                                    ACT.Gelu, bias=col[:, C_B1 + e * FB + j:C_B1 + e * FB + j + 1],
                                                    scale=1.0 / (S_X * S_WT))
                    last.then_inc(up_ok, 1)
                elif name == "turn3":
                    t, = a
                    act.wait_ge(T3_ps, t + 1)
                    if t >= 2:
                        act.wait_ge(q_ps, t - 1)
                    nc.scalar.copy(xT3[:, t % 2, :], T3).then_inc(T3_ok, 1)
                elif name == "query":
                    t, = a
                    act.wait_ge(q_ps, t + 1)
                    if t >= 2:
                        act.wait_ge(eprod_ok, t - 1)
                        act.wait_ge(eprod2_ok, t - 1)
                    nc.scalar.copy(q_sb[:, t % 2, :], Q).then_inc(q_ok, 1)
                elif name == "esum":
                    t, = a
                    act.wait_ge(sub_ok, t + 1)
                    if t >= 2:
                        act.wait_ge(vprod_ok, t - 1)
                        act.wait_ge(vprod2_ok, t - 1)
                        act.wait_ge(soft_ok, t - 1)
                    nc.scalar.activation(pr[:, t % 2, :, :], en[:, t % 2, :, :], ACT.Exp,
                                         scale=INV_SQRT_D).then_inc(exp_ok, 1)
                elif name == "turn5":
                    t, = a
                    act.wait_ge(T5_ps, t + 1)
                    if t >= 2:
                        act.wait_ge(low_ps, t - 1)
                    nc.scalar.copy(xT5[:, t % 2, :], T5).then_inc(T5_ok, 1)
                elif name == "up1":
                    t, = a
                    act.wait_ge(up1_ps, t + 1)
                    if t >= 2:
                        act.wait_ge(y_ps, t - 1)
                    for j in range(FB):
                        last = nc.scalar.activation(hid1[:, t % 2, j, :], ps_h1[:, j * P:(j + 1) * P], ACT.Gelu,
                                                    bias=col[:, C_L1B1 + j:C_L1B1 + j + 1])
                    last.then_inc(hid1_ok, 1)
                elif name == "low2":
                    t, = a
                    act.wait_ge(low_ps, t + 1)
                    if t >= 2:
                        act.wait_ge(y_ps, t - 1)
                    nc.scalar.copy(low[:, t % 2, :], ps_h1[0:FB * NL, 0:P]).then_inc(low_ok, 1)

        @block.vector
        def _(dve):
            def stats(i, tiles, source, ready, count):
                if ready is not None:
                    dve.wait_ge(ready, count)
                for t in tiles:
                    last = nc.vector.bn_stats(bn[:, t, :], source(t))
                last.then_inc(bn_ok[i], 1)
                call = tiles[0] // len(tiles) + 1
                dve.wait_ge(bn_ok[i], call)
                for t in tiles:
                    last = nc.vector.bn_aggr(mv[:, i, t, :], bn[:, t, :])
                last.then_inc(aggr_ok[i], 1)
                dve.wait_ge(aggr_ok[i], call)
                a, b = tiles[0], tiles[-1] + 1
                nc.vector.tensor_scalar(ve[:, i, a:b], mv[:, i, a:b, 1], EPS, None, ALU.add).then_inc(ve_ok[i], 1)

            def norm(i, tiles, source, target):
                dve.wait_ge(rstd_ok[i], tiles[0] // len(tiles) + 1)
                for t in tiles:
                    last = nc.vector.tensor_scalar(target(t), source(t), mv[:, i, t, 0:1], rstd[:, i, t:t + 1],
                                                   ALU.subtract, ALU.mult)
                last.then_inc(norm_ok[i], 1)

            def x_tile(t):
                return x[:, t, :]

            def xn_tile(t):
                return xn[:, t, :]

            nc.vector.memset(src[:, :, 0:SCAN:SEG], 0.0)
            nc.vector.memset(live[:, :], 1.0)
            nc.vector.memset(before[:, :, 0:1], 0.0).then_inc(masks, 1)
            dve.wait_ge(zeroed, 2)
            nc.vector.memset(decay[:, 0:SCAN:SEG], 0.0).then_inc(masks, 1)
            dve.wait_ge(masks, 2)
            dve.wait_ge(ew_ok, 1)
            nc.vector.tensor_scalar(decay[:, :], decay[:, :], ew[:, 0:1], None, ALU.mult).then_inc(decay_ok, 1)
            dve.wait_ge(decay_ok, 1)

            def scans(g):
                dve.wait_ge(ek_ok, g + 1)
                nc.vector.tensor_tensor(seg(src, 0, g, 1), seg(src, 1, g, 1),
                                        ctxT_sb[:, :].rearrange("p (b s) -> p b s", s=P)[:, g * GT:(g + 1) * GT, :],
                                        ALU.mult).then_inc(ekv_ok, 1)
                a, b = g * GT * SEG, (g + 1) * GT * SEG
                back = slice(b, a, -1)
                for s in (1, 0):
                    if s == 0:
                        dve.wait_ge(ekv_ok, g + 1)
                    nc.vector.tensor_tensor_scan(fwd[:, s, a:b], decay[:, a:b], src[:, s, a:b], 0.0,
                                                 ALU.mult, ALU.add)
                    last = nc.vector.tensor_tensor_scan(bwd[:, s, back], decay[:, back], src[:, s, back], 0.0,
                                                        ALU.mult, ALU.add)
                last.then_inc(scan_ok, 1)

            def mixer(g):
                ts = slice(g * GT, (g + 1) * GT)
                m = mixed[:, g % 2, :]
                dve.wait_ge(mix_ps, g + 1)
                dve.wait_ge(er_ok, (g + 1) * GT)
                dve.wait_ge(tg_ok, 1)
                if g >= 2:
                    dve.wait_ge(x1_ok, g - 1)
                nc.vector.scalar_tensor_tensor(m, on[:, ts, :].rearrange("p b d -> p (b d)"), 1.0,
                                               ps_den[:, 0:GT * D], ALU.add, ALU.mult).then_inc(dn_ok, 1)
                dve.wait_ge(dn_ok, g + 1)
                nc.vector.reciprocal(m, m).then_inc(rec_ok, 1)
                dve.wait_ge(rec_ok, g + 1)
                nc.vector.scalar_tensor_tensor(m, ps_num[:, 0:GT * D], tg[:, G_X0:G_X0 + 1], m,
                                               ALU.mult, ALU.mult).then_inc(mixed_ok, 1)
                dve.wait_ge(mixed_ok, g + 1)
                xg = x[:, ts, :].rearrange("p b d -> p (b d)")
                nc.vector.tensor_tensor(xg, xg, m, ALU.add).then_inc(x1_ok, 1)

            scans(0)
            dve.wait_ge(ld_x, 16)
            stats(0, list(range(NB)), x_tile, None, 0)
            scans(1)
            dve.wait_ge(rstd_ok[0], 1)
            nc.vector.tensor_scalar(neg_rstd[:, :], rstd[:, 0, :], -1.0, None, ALU.mult)
            nc.vector.tensor_tensor(mu_rstd[:, :], rstd[:, 0, :], mv[:, 0, :, 0], ALU.mult).then_inc(norm_ok[0], 1)
            dve.wait_ge(wr_step, 1)
            nc.vector.scalar_tensor_tensor(wr[:, 1, :], sw[:, S_R:S_R + NE], S_WT, wr[:, 0, :],
                                           ALU.mult, ALU.subtract).then_inc(wr_step, 1)
            for name, *a in DVE_ORDER:
                if name == "mix":
                    mixer(a[0])
                elif name == "scan" and a[0] >= 2:
                    scans(a[0])
                elif name == "stat1":
                    g, = a
                    stats(1, list(range(g * GT, g * GT + GT)), x_tile, x1_ok, g + 1)
                elif name == "rows":
                    g, = a
                    norm(1, list(range(g * GT, g * GT + GT)), x_tile, xn_tile)
                elif name == "xlow":
                    g, = a
                    dve.wait_ge(xhigh_ok, g + 1)
                    nc.vector.scalar_tensor_tensor(
                        xnT[:, 1, g * GT:(g + 1) * GT, :].rearrange("p b t -> p (b t)"), ps_turn[:, 0:GT * P], S_X,
                        xnT[:, 0, g * GT:(g + 1) * GT, :].rearrange("p b t -> p (b t)"),
                        ALU.mult, ALU.subtract).then_inc(xnT_ok, 1)
                elif name == "choose":
                    dve.wait_ge(logit_ps, NG)
                    nc.vector.tensor_scalar(logit[:, :, :].rearrange("p b e -> p (b e)"), ps_logit[:, 0:NB * NE],
                                            1.0 / (S_X * S_WT), None, ALU.mult).then_inc(logit_ok, 1)
                    dve.wait_ge(logit_ok, 1)
                    for t in range(NB):
                        last = nc.vector.max(top[:, t, :], logit[:, t, :])
                    last.then_inc(ch, 1)
                    dve.wait_ge(ch, 1)
                    for t in range(NB):
                        last = nc.vector.max_index(topi[:, t, :], top[:, t, :], logit[:, t, :])
                    last.then_inc(ch, 1)
                    nc.vector.tensor_tensor(gap[:, :], top[:, :, 1], top[:, :, 0], ALU.subtract).then_inc(ch, 1)
                    dve.wait_ge(ch, 3)
                    nc.vector.tensor_copy(topf[:, :, :], topi[:, :, 0:2]).then_inc(ch, 1)
                    dve.wait_ge(ch, 4)
                    dve.wait_ge(consts, 1)
                    for i in range(2):
                        last = nc.vector.tensor_tensor(
                            hot[:, i, :, :], iota_e[:, :].unsqueeze(1).broadcast_to([P, NB, NE]),
                            topf[:, :, i:i + 1].broadcast_to([P, NB, NE]), ALU.is_equal)
                    last.then_inc(ch, 1)
                    dve.wait_ge(ch, 5)
                    nc.vector.tensor_tensor(assign[:, :, :], hot[:, 0, :, :], hot[:, 1, :, :],
                                            ALU.add).then_inc(ch, 1)
                elif name == "choose2":
                    dve.wait_ge(egap_ok, 1)
                    nc.vector.tensor_scalar(den2[:, :], egap[:, :], 1.0, None, ALU.add).then_inc(ch, 1)
                    dve.wait_ge(ch, 7)
                    nc.vector.reciprocal(wt[:, 0, :], den2[:, :]).then_inc(ch, 1)
                    dve.wait_ge(ch, 8)
                    nc.vector.tensor_tensor(wt[:, 1, :], wt[:, 0, :], egap[:, :], ALU.mult).then_inc(ch, 1)
                    dve.wait_ge(ch, 9)
                    for i in range(2):
                        last = nc.vector.tensor_tensor(
                            hot[:, i, :, :], hot[:, i, :, :],
                            wt[:, i, :].unsqueeze(2).broadcast_to([P, NB, NE]), ALU.mult)
                    last.then_inc(ch, 1)
                    dve.wait_ge(ch, 10)
                    nc.vector.tensor_tensor(weight[:, :, :], hot[:, 0, :, :], hot[:, 1, :, :],
                                            ALU.add).then_inc(ch, 1)
                    dve.wait_ge(ch, 11)
                    dve.wait_ge(tg_ok, 1)
                    nc.vector.tensor_scalar(weight[:, :, :], weight[:, :, :], tg[:, G_F0:G_F0 + 1], None,
                                            ALU.mult).then_inc(ch, 1)
                    dve.wait_ge(ch, 12)
                elif name == "rank":
                    e, = a
                    dve.wait_ge(rk, 2 * e) if e else dve.wait_ge(masks, 2)
                    nc.vector.tensor_tensor(elig[:, e, :], assign[:, :, e], live[:, :], ALU.mult).then_inc(elig_ok, 1)
                    dve.wait_ge(elig_ok, 2 * e + 1)
                    nc.vector.tensor_tensor_scan(before[:, e, 1:NB + 1], one8[:, :], elig[:, e, :], 0.0,
                                                 ALU.mult, ALU.add).then_inc(elig_ok, 1)
                    dve.wait_ge(rank_ps, e + 1)
                    nc.vector.scalar_tensor_tensor(over[:, :], ps_rank[:, e * NB:(e + 1) * NB],
                                                   float(CAP), elig[:, e, :], ALU.is_gt, ALU.mult).then_inc(rk, 1)
                    dve.wait_ge(rk, 2 * e + 1)
                    nc.vector.tensor_tensor(live[:, :], live[:, :], over[:, :], ALU.subtract).then_inc(rk, 1)
                elif name == "coef":
                    dve.wait_ge(rk, 2 * NE)
                    nc.vector.tensor_tensor(coef[:, :, 0:NE], weight[:, :, :],
                                            live[:, :].unsqueeze(2).broadcast_to([P, NB, NE]), ALU.mult)
                    nc.vector.tensor_scalar(over[:, :], live[:, :], -1.0, 1.0, ALU.mult, ALU.add).then_inc(rk, 1)
                    dve.wait_ge(rk, 2 * NE + 1)
                    nc.vector.tensor_scalar(coef[:, :, FALL], over[:, :], tg[:, G_F0:G_F0 + 1], None,
                                            ALU.mult).then_inc(coef_ok, 1)
                    for g in range(NG):
                        dve.wait_ge(coefT_ps, g + 1)
                        nc.vector.tensor_copy(coefT[:, g * GT:(g + 1) * GT, :].rearrange("p b t -> p (b t)"),
                                              ps_turn[0:NF, 0:GT * P]).then_inc(coefT_ok, 1)
                elif name == "down":
                    c, = a
                    dve.wait_ge(down_ps, c + 1)
                    dve.wait_ge(coef_ok, 1)
                    for n in range(c * CHUNK, (c + 1) * CHUNK):
                        t, e = TERMS[n]
                        if n:
                            dve.wait_ge(sum_ok, n)
                        nc.vector.scalar_tensor_tensor(x[:, t, :], place(n),
                                                       1.0 if e is None else coef[:, t, e:e + 1], x[:, t, :],
                                                       ALU.mult, ALU.add).then_inc(sum_ok, 1)
                elif name == "stat3":
                    t, = a
                    stats(2, [t], x_tile, sum_ok, NTERM * (t + 1))
                elif name == "norm3":
                    norm(2, [a[0]], x_tile, xn_tile)
                elif name == "eprod":
                    query_key_products(nc.vector, dve, a[0], HG, NH, eprod2_ok)
                elif name == "vprod":
                    weight_value_products(nc.vector, dve, a[0], HG, NH, vprod2_ok)
                elif name == "esum":
                    t, = a
                    dve.wait_ge(eprod_ok, t + 1)
                    dve.wait_ge(eprod2_ok, t + 1)
                    if t >= 2:
                        dve.wait_ge(exp_ok, t - 1)
                    e2 = en[:, t % 2, :, :]
                    nc.vector.tensor_reduce(e2.rearrange("p h g -> p (h g)"),
                                            eprod[t % 2].rearrange("p (e d) -> p e d", d=DH), AX_X,
                                            ALU.add).then_inc(ered_ok, 1)
                    dve.wait_ge(ered_ok, t + 1)
                    nc.vector.tensor_reduce(mx[:, t % 2, :], e2, AX_X, ALU.max).then_inc(max_ok, 1)
                    dve.wait_ge(max_ok, t + 1)
                    nc.vector.tensor_tensor(e2, e2, mx[:, t % 2, :].unsqueeze(2).broadcast_to([P, NH, NH]),
                                            ALU.subtract).then_inc(sub_ok, 1)
                elif name == "soft":
                    t, = a
                    dve.wait_ge(exp_ok, t + 1)
                    nc.vector.tensor_reduce(sm[:, t % 2, :], pr[:, t % 2, :, :], AX_X, ALU.add).then_inc(soft_ok, 1)
                    dve.wait_ge(soft_ok, t + 1)
                    nc.vector.reciprocal(rs[:, t % 2, :], sm[:, t % 2, :]).then_inc(rs_ok, 1)
                elif name == "vsum":
                    t, = a
                    dve.wait_ge(vprod_ok, t + 1)
                    dve.wait_ge(vprod2_ok, t + 1)
                    nc.vector.tensor_reduce(att[:, t % 2, :], vprod.rearrange("p (e g) -> p e g", g=NH), AX_X,
                                            ALU.add).then_inc(vred_ok, 1)
                    dve.wait_ge(vred_ok, t + 1)
                    dve.wait_ge(rs_ok, t + 1)
                    av = att[:, t % 2, :].rearrange("p (h d) -> p h d", d=DH)
                    nc.vector.tensor_tensor(av, av, rs[:, t % 2, :].unsqueeze(2).broadcast_to([P, NH, DH]),
                                            ALU.mult).then_inc(att_ok, 1)
                    stats(3, [t], lambda t: att[:, t % 2, :], att_ok, t + 1)
                elif name == "norm4":
                    norm(3, [a[0]], lambda t: att[:, t % 2, :], lambda t: on[:, t, :])
                elif name == "turn4":
                    t, = a
                    dve.wait_ge(T4_ps, t + 1)
                    if t >= 2:
                        dve.wait_ge(wo_ps, t - 1)
                    nc.vector.tensor_scalar(oT[:, t % 2, :], T4, col[:, C_LNG:C_LNG + 1], col[:, C_LNB:C_LNB + 1],
                                            ALU.mult, ALU.add).then_inc(oT_ok, 1)
                elif name == "wo":
                    t, = a
                    dve.wait_ge(wo_ps, t + 1)
                    nc.vector.scalar_tensor_tensor(x[:, t, :], WO, tg[:, G_X1:G_X1 + 1], x[:, t, :],
                                                   ALU.mult, ALU.add).then_inc(x3_ok, 1)
                elif name == "stat5":
                    stats(4, [a[0]], x_tile, x3_ok, a[0] + 1)
                elif name == "norm5":
                    norm(4, [a[0]], x_tile, xn_tile)
                elif name == "lora":
                    t, = a
                    if t == 0:
                        dve.wait_ge(ld_gate, 16)
                        nc.vector.tensor_scalar(mask_s[:, :, :], mask_s[:, :, :],
                                                gate[0:NL, G_SCALE:G_SCALE + 1], None, ALU.mult).then_inc(mask_ok, 1)
                        nc.vector.tensor_scalar(mask16[:, :, :], mask16[:, :, :],
                                                gate[0:FB * NL, G_SCALE:G_SCALE + 1], None,
                                                ALU.mult).then_inc(mask_ok, 1)
                        dve.wait_ge(mask_ok, 2)
                    if t >= 2:
                        dve.wait_ge(y_ps, t - 1)
                    dve.wait_ge(T5_ok, t + 1)
                    nc.vector.tensor_copy(
                        odd2[:, t % 2, :].rearrange("p (r s) -> p r s", r=FB)[:, :, 0:NL],
                        xT5[:, t % 2, 2 + 2 * NL:2 + 4 * NL:2].unsqueeze(1).broadcast_to([P, FB, NL])
                        ).then_inc(odd2_ok, 1)
                    dve.wait_ge(fac_ps, t + 1)
                    nc.vector.tensor_copy(even1[:, t % 2, :], EVEN1)
                    nc.vector.tensor_tensor(u_mask[:, t % 2, :, :], U1.unsqueeze(1).broadcast_to([NL, NL, P]),
                                            mask_s[:, :, :], ALU.mult)
                    nc.vector.tensor_tensor(even2[:, t % 2, :, :],
                                            EVEN2.unsqueeze(1).broadcast_to([FB * NL, NL, P // NL]),
                                            mask16[:, :, :], ALU.mult).then_inc(fac_ok, 1)
                elif name == "down1":
                    t, = a
                    dve.wait_ge(y_ps, t + 1)
                    nc.vector.scalar_tensor_tensor(x[:, t, :], Y5, tg[:, G_F1:G_F1 + 1], x[:, t, :],
                                                   ALU.mult, ALU.add).then_inc(y_ok, 1)

        @block.tensor
        def _(pe):
            mm = nc.tensor.matmul

            def bank_free(*item):
                n = WORK.index(item) - NWORK
                if n < 0:
                    return
                kind, *b = WORK[n]
                if kind == "kv":
                    pe.wait_ge(kv_ok, b[0] + 1)
                elif kind == "up":
                    pe.wait_ge(up_ok, NTH_UP[b[0], b[1]] * PAIRS + b[2] + 1)
                else:
                    pe.wait_ge(sum_ok, (b[0] + 1) * CHUNK)

            def project(dst, lhsT, w0, r0, n):
                mm(dst, lhsT, sw[:, w0:w0 + n], start=True, stop=False)
                return mm(dst, ones3[:, :], row3[:, r0:r0 + n], start=False, stop=True)

            def three(dst, parts_a, parts_b):
                mm(dst, parts_a[0], parts_b[0], start=True, stop=False)
                mm(dst, parts_a[0], parts_b[1], start=False, stop=False)
                return mm(dst, parts_a[1], parts_b[0], start=False, stop=True)

            for name, *a in PE_ORDER:
                if name == "kv":
                    if a[0] == 0:
                        pe.wait_ge(ld_ctx, 16)
                        pe.wait_ge(ld_small, 16)
                        pe.wait_ge(row3_ok, 48)
                        pe.wait_ge(consts, 2)
                    for t in range(a[0] * GT, a[0] * GT + GT):
                        bank_free("kv", t)
                        project(work_bank("kv", t)[:, 0:2 * D], ctxT_sb[:, t * P:(t + 1) * P], S_KV, R_KV, 2 * D).then_inc(kv_ps, 1)
                elif name == "mix":
                    g, = a
                    pe.wait_ge(scan_ok, g + 1)
                    pe.wait_ge(diag_ok, 1)
                    if g:
                        pe.wait_ge(mixed_ok, g)
                    for s, dst in ((1, ps_den), (0, ps_num)):
                        for i in range(GT):
                            o = (g * GT + i) * SEG
                            d = dst[:, i * D:(i + 1) * D]
                            mm(d, fwd[:, s, o:o + P], ident[:, :], start=True, stop=False)
                            mm(d, bwd[:, s, o + 2:o + 2 + P], ident[:, :], start=False, stop=False)
                            last = mm(d, src[:, s, o + 1:o + 1 + P], diag_u[:, :], start=False, stop=True)
                    last.then_inc(mix_ps, 1)
                elif name == "rows":
                    g, = a
                    pe.wait_ge(norm_ok[1], g + 1)
                    if g:
                        pe.wait_ge(xnT_ok, g)
                    for i in range(GT):
                        last = nc.tensor.transpose(ps_turn[:, i * P:(i + 1) * P], xn[:, g * GT + i, :], ident[:, :])
                    last.then_inc(turn_ps, 1)
                elif name == "logits":
                    g, = a
                    pe.wait_ge(xnT_ok, g + 1)
                    pe.wait_ge(wr_step, 2)
                    for t in range(g * GT, g * GT + GT):
                        last = three(ps_logit[:, t * NE:(t + 1) * NE], (xnT[:, 0, t, :], xnT[:, 1, t, :]),
                                     (wr[:, 0, :], wr[:, 1, :]))
                    last.then_inc(logit_ps, 1)
                elif name == "rank":
                    e, = a
                    d = ps_rank[:, e * NB:(e + 1) * NB]
                    pe.wait_ge(elig_ok, 2 * e + 2)
                    mm(d, tri[:, :], elig[:, e, :], start=True, stop=False)
                    mm(d, ones_bf[:, :], before[:, e, 0:NB], start=False, stop=True).then_inc(rank_ps, 1)
                elif name == "coef":
                    pe.wait_ge(coef_ok, 1)
                    for g in range(NG):
                        pe.wait_ge(coefT_ok, g) if g else pe.wait_ge(xnT_ok, NG)
                        for i in range(GT):
                            last = nc.tensor.transpose(ps_turn[0:NF, i * P:(i + 1) * P], coef[:, g * GT + i, :],
                                                       ident[:, :])
                        last.then_inc(coefT_ps, 1)
                elif name == "up":
                    g, e, i = a
                    if i == 0:
                        pe.wait_ge(split_ok, FFNS.index(e) + 1)
                        pe.wait_ge(xnT_ok, g + 1)
                    bank_free("up", g, e, i)
                    ts = slice(g * GT, (g + 1) * GT)
                    rows = [xnT[:, k, ts, :].rearrange("p b t -> p (b t)") for k in range(2)]
                    for k in range(2):
                        c = slice((2 * i + k) * P, (2 * i + k + 1) * P)
                        last = three(work_bank("up", g, e, i)[:, k * GT * P:(k + 1) * GT * P],
                                     (wu[:, 0, e, c], wu[:, 1, e, c]), rows)
                    last.then_inc(up_ps, 1)
                elif name == "down":
                    c, = a
                    bank_free("down", c)
                    for n in range(c * CHUNK, (c + 1) * CHUNK):
                        t, e = TERMS[n]
                        if e is None:
                            pe.wait_ge(ld_b2, 16)
                            pe.wait_ge(coefT_ok, NG)
                            last = mm(place(n), coefT[:, t, :], b2_sb[:, :], start=True, stop=True)
                            continue
                        pe.wait_ge(ld_dn[e], 16)
                        pe.wait_ge(up_ok, (NTH_UP[t // GT, e] + 1) * PAIRS)
                        for j in range(FB):
                            last = mm(place(n), hid[:, t // GT % 2, e, j, t % GT * P:(t % GT + 1) * P], wd[:, e, j, :],
                                      start=(j == 0), stop=(j == FB - 1))
                    last.then_inc(down_ps, 1)
                elif name == "turn3":
                    t, = a
                    pe.wait_ge(norm_ok[2], t + 1)
                    if t:
                        pe.wait_ge(q_ok, t)
                    nc.tensor.transpose(T3, xn[:, t, :], ident[:, :]).then_inc(T3_ps, 1)
                elif name == "query":
                    t, = a
                    pe.wait_ge(T3_ok, t + 1)
                    project(Q, xT3[:, t % 2, :], S_Q, R_Q, D).then_inc(q_ps, 1)
                elif name == "turn4":
                    t, = a
                    pe.wait_ge(norm_ok[3], t + 1)
                    if t:
                        pe.wait_ge(x3_ok, t)
                    nc.tensor.transpose(T4, on[:, t, :], ident[:, :]).then_inc(T4_ps, 1)
                elif name == "wo":
                    t, = a
                    pe.wait_ge(oT_ok, t + 1)
                    project(WO, oT[:, t % 2, :], S_O, R_O, D).then_inc(wo_ps, 1)
                elif name == "turn5":
                    t, = a
                    pe.wait_ge(norm_ok[4], t + 1)
                    if t:
                        pe.wait_ge(fac_ok, t)
                    nc.tensor.transpose(T5, xn[:, t, :], ident[:, :]).then_inc(T5_ps, 1)
                elif name == "lora":
                    t, = a
                    pe.wait_ge(T5_ok, t + 1)
                    mm(EVEN1, ident[:, 1:1 + 2 * NL:2], xn[:, t, :], start=True, stop=True)
                    for r in range(FB):
                        mm(EVEN2, pick[:, r, :], xn[:, t, r:D:FB], start=(r == 0), stop=(r == FB - 1))
                    mm(U1, xT5[:, t % 2, 2:2 + 2 * NL:2], xT5[:, t % 2, :],
                       start=True, stop=True).then_inc(fac_ps, 1)
                elif name == "up1":
                    t, = a
                    pe.wait_ge(fac_ok, t + 1)
                    pe.wait_ge(ld_l1, 32)
                    if t:
                        pe.wait_ge(low_ok, t)
                    for j in range(FB):
                        d = ps_h1[:, j * P:(j + 1) * P]
                        mm(d, w1u[:, j * P:(j + 1) * P], xT5[:, t % 2, :], start=True, stop=False)
                        last = mm(d, even1[:, t % 2, :], u_mask[:, t % 2, j, :], start=False, stop=True)
                    last.then_inc(up1_ps, 1)
                elif name == "low2":
                    t, = a
                    pe.wait_ge(hid1_ok, t + 1)
                    pe.wait_ge(odd2_ok, t + 1)
                    for r in range(FB):
                        last = mm(ps_h1[0:FB * NL, 0:P], odd2[:, t % 2, r * FB * NL:(r + 1) * FB * NL],
                                  hid1[:, t % 2, r, :], start=(r == 0), stop=(r == FB - 1))
                    last.then_inc(low_ps, 1)
                elif name == "down1":
                    t, = a
                    pe.wait_ge(low_ok, t + 1)
                    if t:
                        pe.wait_ge(y_ok, t)
                    for r in range(FB):
                        mm(Y5, hid1[:, t % 2, r, :], w1d[:, r, :], start=(r == 0), stop=False)
                    mm(Y5, low[:, t % 2, :], even2[:, t % 2, :, :].rearrange("p j o -> p (j o)"),
                       start=False, stop=False)
                    mm(Y5, ones3[:, :], row3[:, R_B2:R_B2 + D], start=False, stop=True).then_inc(y_ps, 1)


def kernel(**inputs):
    import numpy as np
    import concourse.bacc as bacc
    from concourse.bass_utils import run_bass_kernel_spmd

    a = {k: np.asarray(v) for k, v in inputs.items()}

    def hidden_cols(b):
        return b.reshape(-1, P).T

    w_up = np.concatenate([a["L0_ffn_W1"], a["L0_ffn_fw1"][None]]).transpose(1, 0, 2)
    w_down = np.concatenate([a["L0_ffn_W2"], a["L0_ffn_fw2"][None]]).reshape(NF, FB, P, D).transpose(2, 0, 1, 3)
    by_dim = a["L1_xattn_Wv"].reshape(NH, DH, D).transpose(1, 0, 2).reshape(D, D)
    arrays = {
        "ctxT": a["ctx_1024"].transpose(2, 0, 1).reshape(D, NB * P),
        "x_in": a["x"].transpose(1, 0, 2).reshape(P, NB * D),
        "cols": np.concatenate([a["L0_xattn_w"].reshape(D, 1), a["L0_xattn_u"].reshape(D, 1),
                                a["L1_xattn_ln_g"].reshape(D, 1), a["L1_xattn_ln_b"].reshape(D, 1),
                                hidden_cols(a["L0_ffn_b1"]), hidden_cols(a["L0_ffn_fb1"]),
                                hidden_cols(a["L1_ffn_b1"])], axis=1),
        "gates": np.stack([a["g_xattn"][0], a["g_ffn"][0], a["g_xattn"][1], a["g_ffn"][1],
                           a["L1_ffn_scale"]]).reshape(1, 5),
        "rows": np.concatenate([a["L1_xattn_bk"], a["L1_xattn_bv"].reshape(NH, DH).T.reshape(D), a["L1_xattn_bq"],
                                a["L1_xattn_bo"], a["L1_ffn_b2"]]).reshape(NROW // D, D),
        "small": np.concatenate([a["L1_xattn_Wk"].T, by_dim.T, a["L1_xattn_Wq"].T, a["L1_xattn_Wo"].T,
                                 a["L0_ffn_Wr"]], axis=1),
        "w_up": w_up,
        "w_down": w_down,
        "b2": np.concatenate([a["L0_ffn_b2"], a["L0_ffn_fb2"][None]]),
        "l1_up": a["L1_ffn_W1"].T,
        "l1_down": a["L1_ffn_W2"].T.reshape(FB, P, D).transpose(1, 0, 2),
    }
    arrays = {k: np.ascontiguousarray(v) for k, v in arrays.items()}
    nc = bacc.Bacc("TRN2", target_bir_lowering=False, num_devices=1)
    aps = [nc.dram_tensor(k, v.shape, mybir.dt.from_np(v.dtype), kind="ExternalInput").ap()
           for k, v in arrays.items()]
    out = nc.dram_tensor("out", (NB, P, D), F32, kind="ExternalOutput").ap()
    flamingo_kernel(nc, *aps, out)
    r = run_bass_kernel_spmd(nc, [arrays], core_ids=[0])
    return r.results[0]["out"]
```

```python
from contextlib import ExitStack

import concourse.bass as bass
from concourse import mybir

P = 128
NB = 8
GT = 2
NG = NB // GT
D = 128
FF = 512
FB = FF // P
NE = 8
FALL = NE
NF = NE + 1
CAP = max(int(1.25 * (4 * 256 * 2 / NE)), 4)
NH = 16
DH = D // NH
NL = 4
EPS = 1e-5
SEG = P + 1
SCAN = NB * SEG + 1
NTERM = NF + 1
CHUNK = 2
PAIRS = FB // 2
POOL_NORMS = (2, 3, 4)
HEADS = (9, 13, 9, 9, 10, 15, 11, 10)
S_X, S_WT = 16.0, 256.0
NSTAGE = 5
NWORK = 3
INV_SQRT_D = float(D) ** -0.5

ALU = mybir.AluOpType
ACT = mybir.ActivationFunctionType
F32 = mybir.dt.float32
BF16 = mybir.dt.bfloat16
F16 = mybir.dt.float16
U32 = mybir.dt.uint32
AX_X = mybir.AxisListType.X

C_W, C_U, C_LNG, C_LNB, C_B1 = 0, 1, 2, 3, 4
C_L1B1 = C_B1 + NF * FB
NCOL = C_L1B1 + FB
S_KV, S_Q, S_O, S_R = 0, 2 * D, 3 * D, 4 * D
NSMALL = 4 * D + NE
R_KV, R_Q, R_O, R_B2 = 0, 2 * D, 3 * D, 4 * D
NROW = 5 * D
G_X0, G_F0, G_X1, G_F1, G_SCALE = range(5)

PIECES = {
    "stat3": (-0.49, -0.93, 0.9, -3.23), "norm3": (3.16, 3.16, 3.22, 3.11), "turn3": (2.47, 1.67, 2.52, 5.14),
    "query": (3.49, 3.44, 3.08, 3.38), "eprod": (4.42, 3.63, 4.51, 1.83), "esum": (6.9, 6.66, 7.74, 6.79),
    "vprod": (9.31, 9.66, 10.43, 9.34), "soft": (13.14, 10.67, 8.08, 12.91), "vsum": (13.44, 13.44, 13.7, 13.21),
    "norm4": (17.78, 17.78, 17.26, 17.48), "turn4": (19.15, 18.27, 18.62, 17.96), "wo": (19.74, 19.74, 16.45, 19.9),
    "stat5": (20.74, 21.81, 21.14, 20.01), "norm5": (27.48, 25.43, 25.92, 25), "turn5": (27.35, 26.68, 27.19, 26.22),
    "lora": (28.58, 28.58, 29.13, 28.05), "up1": (32.48, 32.55, 32.85, 31.93), "low2": (36.11, 36.11, 37.25, 33.98),
    "down1": (43.63, 43.46, 44.47, 42.9),
}
LAST_TILES = 2
PIECES_LAST = {
    "stat3": (-6.26, -0.93, -1.02, -0.87), "norm3": (2.86, 3.55, 3.04, 1.96), "turn3": (2.85, -0.7, 2.99, 5.25),
    "query": (4.45, 2.95, 3.22, 2.79), "eprod": (4.54, 4.45, 4.84, 1.76), "esum": (6.49, 5.39, 7.69, 5.93),
    "vprod": (8.53, 8.32, 9.19, 7.74), "soft": (11.97, 9.2, 7.09, 11.02), "vsum": (13.2, 12.88, 15.06, 12.14),
    "norm4": (20.11, 19.75, 21.78, 18.63), "turn4": (21.5, 20.11, 21.66, 19.08), "wo": (22.28, 21.75, 21.12, 21.13),
    "stat5": (24.76, 23.33, 27.1, 23.06), "norm5": (32.07, 28.77, 21.72, 27.11),
    "turn5": (31.63, 30.27, 32.53, 28.77), "lora": (32.16, 31.92, 34.31, 30.35), "up1": (40.61, 39.78, 47, 38.42),
    "low2": (44.76, 43.83, 47, 43.13), "down1": (50.29, 49.9, 52.91, 46.83),
}
START = {
    ("constants",): (-4.63, -4.44, -4.63, -7.65), ("bias",): (-2.7, 0, 0, -9.3),
    ("split", FALL): (-1.46, -4.9, -8, 0), ("split", 0): (0, -3.79, -7.3, 0), ("split", 1): (0, -2.8, -6.2, 0),
    ("split", 2): (0, -1.84, -5.9, 0), ("split", 3): (0, 0.6, -5.2, 0), ("split", 4): (0, 1.2, -0.69, 0),
    ("split", 5): (0, 2.2, -0.1, 0), ("split", 6): (0, 4.38, 0, 0), ("split", 7): (3.22, 6.87, 5.12, 3.05),
    ("mix", 0): (-13.91, -8.09, -8.22, -8.91), ("stat1", 0): (-1.27, -5.97, -1.27, -5.97),
    ("rows", 0): (-2.5, -3.2, -2.4, -3.91), ("xlow", 0): (0, -0.4, 0, 0), ("logits", 0): (2.04, -0.93, 1.8, 1.8),
    ("kv", 0): (-4.4, 0, -4.2, 0), ("mix", 1): (-9, -5, -4, -4), ("stat1", 1): (0, -0.7, 0, -0.7),
    ("rows", 1): (1.43, -0.18, 1.14, 0.42), ("xlow", 1): (0, 1.8, 0, 0), ("logits", 1): (5.6, 4.31, 3.52, 2.19),
    ("kv", 1): (-2.5, 0, -3.74, 0), ("scan", 2): (-1.59, -8.09, -1.59, -1.59), ("mix", 2): (-4.5, 1.47, 2.06, 0),
    ("stat1", 2): (0, 2.4, 0, 2.8), ("rows", 2): (5.49, 4.02, 4.82, 3.52), ("xlow", 2): (0, 5.79, 0, 0),
    ("logits", 2): (6.5, 7.33, 6.5, 6.5), ("kv", 2): (-1.4, 0, -1.2, 0), ("scan", 3): (-0.19, -2.7, 0.8, 0.8),
    ("mix", 3): (-0.42, 3.58, 4.58, 4.58), ("stat1", 3): (2.23, 5.78, 0.78, 5.88),
    ("rows", 3): (7.5, 6.8, 6.74, 5.73), ("xlow", 3): (5.1, 7.8, 0, 0), ("logits", 3): (8.32, 8.24, 8.24, 8.24),
    ("kv", 3): (2.11, 0.25, 2.46, 0.25), ("choose",): (8.5, 8.5, 8.5, 8.5), ("choose2",): (11.5, 10.58, 10.34, 10.58),
    ("rank", 0): (10.6, 9, 20, 20), ("rank", 1): (11.05, 10.05, 20, 20), ("rank", 2): (12.09, 11.1, 20, 20),
    ("rank", 3): (12.84, 12.15, 20, 20), ("rank", 4): (13.57, 13.2, 20, 20), ("rank", 5): (14.74, 14.25, 20, 20),
    ("rank", 6): (16.3, 14.52, 20, 20), ("rank", 7): (17.43, 17.15, 20.69, 20.69), ("coef",): (20, 19, 19.29, 19),
    ("turn", 0): (26, 0, 26, -3.3), ("turn", 1): (28, 0, 28, 0), ("turn", 2): (30, 0, 31.07, 0),
    ("turn", 3): (32, 1.12, 32, 0),
}
T_UP, T_DOWN = 0.518, 1.7
SPREAD = 0.5
T_COEF = 22.79
FFNS = (FALL, *range(NE))


def timeline(engine):
    items = []
    at = 0.0

    def put(when, *item):
        items.append((when, len(items), item))

    def up(g, ffns):
        nonlocal at
        for e in ffns:
            for i in range(PAIRS):
                put(at, "up", g, e, i)
                at += T_UP

    def down(c):
        nonlocal at
        put(at, "down", c)
        at += T_DOWN
        t, last = divmod(c + 1, NTERM // CHUNK)
        if last == 0:
            for piece, lags in (PIECES if t <= NB - LAST_TILES else PIECES_LAST).items():
                put(at + lags[engine], piece, t - 1)

    for item, lags in START.items():
        put(lags[engine], *item)
    up(0, FFNS)
    up(1, FFNS)
    at = max(at, T_COEF)
    per_group = GT * NTERM // CHUNK
    ups = sorted((per_group * g + per_group // GT + SPREAD * (i - 1), g + 2, e)
                 for g in range(NG - 2) for i, e in enumerate(FFNS))
    for c in range(NG * per_group):
        down(c)
        while ups and ups[0][0] <= c:
            _, g, e = ups.pop(0)
            up(g, [e])
    return [item for _, _, item in sorted(items, key=lambda x: x[:2])]


NTH_UP = {(g, e): g * NF + i for g in range(NG) for i, e in enumerate(FFNS)}
TERMS = [(t, e) for t in range(NB) for e in (*FFNS, None)]
PE_ORDER, DVE_ORDER, ACT_ORDER, POOL_ORDER = (timeline(i) for i in range(4))
WORK = [("kv", t) if item[0] == "kv" else item for item in PE_ORDER if item[0] in ("kv", "up", "down")
        for t in (range(item[1] * GT, item[1] * GT + GT) if item[0] == "kv" else (0,))]


def flamingo_kernel(nc, ctxT, x_in, cols, gates, rows, small, w_up, w_down, b2, l1_up, l1_down, out):
    with ExitStack() as ctx:
        def sb(name, shape, dt=F32):
            return ctx.enter_context(nc.sbuf_tensor(name, shape, dt))

        def bank(name):
            return ctx.enter_context(nc.psum_tensor(name, [P, 512], F32))

        def sem(name):
            return ctx.enter_context(nc.semaphore(name))

        ctxT_sb = sb("ctxT_sb", [P, NB * P])
        x = sb("x", [P, NB, D])
        xn = sb("xn", [P, NB, D])
        col = sb("col", [P, NCOL])
        gate = sb("gate", [P, 5])
        tg = sb("tg", [P, 4])
        row5 = sb("row5", [NROW // D, D])
        row_part = sb("row_part", [NROW // D, 3, D], BF16)
        row3 = sb("row3", [3, NROW], BF16)
        sw = sb("sw", [P, NSMALL])
        w_stage = sb("w_stage", [P, NSTAGE, FF])
        wu = sb("wu", [P, 2, NF, FF], F16)
        wr = sb("wr", [P, 2, NE], F16)
        wd = sb("wd", [P, NF, FB, D])
        b2_sb = sb("b2_sb", [NF, D])
        w1u = sb("w1u", [P, FF])
        w1d = sb("w1d", [P, FB, D])
        ew = sb("ew", [P, 2])
        decay = sb("decay", [P, SCAN])
        src = sb("src", [P, 2, SCAN])
        fwd = sb("fwd", [P, 2, SCAN])
        bwd = sb("bwd", [P, 2, SCAN])
        diag_u = sb("diag_u", [P, P])
        ident = sb("ident", [P, P])
        tri = sb("tri", [P, P], BF16)
        ones_bf = sb("ones_bf", [P, P], BF16)
        ones3 = sb("ones3", [3, P], BF16)
        iota_e = sb("iota_e", [P, NE])
        minus_half = sb("minus_half", [P, NB])
        one8 = sb("one8", [P, NB])
        mask_s = sb("mask_s", [NL, NL, P])
        mask16 = sb("mask16", [FB * NL, NL, P // NL])
        pick = sb("pick", [P, FB, FB * NL])
        on = sb("on", [P, NB, D])
        mixed = sb("mixed", [P, 2, GT * D])
        bn = sb("bn", [P, NB, 6])
        mv = sb("mv", [P, 5, NB, 2])
        ve = sb("ve", [P, 5, NB])
        rstd = sb("rstd", [P, 5, NB])
        neg_rstd = sb("neg_rstd", [P, NB])
        mu_rstd = sb("mu_rstd", [P, NB])
        xnT = sb("xnT", [P, 2, NB, P], F16)
        hid = sb("hid", [P, 2, NF, FB, GT * P])
        k_sb = sb("k_sb", [P, NB, D])
        v_sb = sb("v_sb", [P, NB, D])
        logit = sb("logit", [P, NB, NE])
        top = sb("top", [P, NB, 8])
        topi = sb("topi", [P, NB, 8], U32)
        topf = sb("topf", [P, NB, 2])
        gap = sb("gap", [P, NB])
        egap = sb("egap", [P, NB])
        den2 = sb("den2", [P, NB])
        wt = sb("wt", [P, 2, NB])
        hot = sb("hot", [P, 2, NB, NE])
        assign = sb("assign", [P, NB, NE])
        weight = sb("weight", [P, NB, NE])
        live = sb("live", [P, NB])
        over = sb("over", [P, NB])
        elig = sb("elig", [P, NE, NB], BF16)
        before = sb("before", [P, NE, NB + 1], BF16)
        coef = sb("coef", [P, NB, NF])
        coefT = sb("coefT", [NF, NB, P])
        q_sb = sb("q_sb", [P, 2, D])
        xT3 = sb("xT3", [P, 2, P])
        oT = sb("oT", [P, 2, P])
        xT5 = sb("xT5", [P, 2, P])
        en = sb("en", [P, 2, NH, NH])
        mx = sb("mx", [P, 2, NH])
        pr = sb("pr", [P, 2, NH, NH])
        sm = sb("sm", [P, 2, NH])
        rs = sb("rs", [P, 2, NH])
        att = sb("att", [P, 2, D])
        odd2 = sb("odd2", [P, 2, FB * (FB * NL + NL)])

        eprod = [fwd[:, :, :].rearrange("p a s -> p (a s)")[:, 0:NH * NH * DH],
                 bwd[:, :, :].rearrange("p a s -> p (a s)")[:, 0:NH * NH * DH]]
        vprod = src[:, :, :].rearrange("p a s -> p (a s)")[:, 0:NH * NH * DH]
        u_mask = decay[0:NL, 0:2 * NL * P].rearrange("p (i j t) -> p i j t", i=2, j=NL)
        hid1 = ctxT_sb[:, :].rearrange("p (i r t) -> p i r t", i=2, r=FB)

        even1 = w_stage[0:NL, 0, 0:2 * P].rearrange("p (i t) -> p i t", i=2)
        low = w_stage[0:FB * NL, 1, 0:2 * P].rearrange("p (i t) -> p i t", i=2)
        even2 = w_stage[0:FB * NL, 2, 0:2 * P].rearrange("p (i j o) -> p i j o", i=2, j=NL)

        work = [bank(f"ps_work{i}") for i in range(NWORK)]
        ps_mix = [bank("ps_mix0"), bank("ps_mix1")]
        ps_turn = bank("ps_turn")
        ps_logit = bank("ps_logit")
        ps_rank = bank("ps_rank")
        ps_q, ps_o, ps_x5, ps_h1, ps_y = *ps_mix, ps_turn, ps_logit, ps_rank
        T3, Q = ps_q[:, 0:P], ps_q[:, P:2 * P]
        T4, WO = ps_o[:, 0:P], ps_o[:, P:2 * P]
        T5, EVEN1, U1, EVEN2 = ps_x5[:, 0:P], ps_x5[0:NL, P:2 * P], ps_x5[0:NL, 2 * P:3 * P], \
            ps_x5[0:FB * NL, 3 * P:3 * P + P // NL]
        Y5 = ps_y[:, 0:D]

        def work_bank(*item):
            return work[WORK.index(item) % NWORK]

        def place(n):
            return work_bank("down", n // CHUNK)[:, n % CHUNK * D:(n % CHUNK + 1) * D]

        def seg(buf, a, g, off):
            v = buf[:, a, off:off + NB * SEG] if off + NB * SEG <= SCAN else None
            return v.rearrange("p (b s) -> p b s", s=SEG)[:, g * GT:(g + 1) * GT, 0:P]

        ld_ctx, ld_x, ld_col, ld_gate, ld_row, ld_small, ld_b2, ld_l1 = (
            sem(f"ld_{n}") for n in ("ctx", "x", "col", "gate", "row", "small", "b2", "l1"))
        ld_up = [sem(f"ld_up{e}") for e in range(NF)]
        ld_dn = [sem(f"ld_dn{e}") for e in range(NF)]
        consts, zeroed, masks, mask_ok = sem("consts"), sem("zeroed"), sem("masks"), sem("mask_ok")
        row_step, row3_ok, high_ok, split_ok, xhigh_ok, odd2_ok = (
            sem(n) for n in ("row_step", "row3_ok", "high_ok", "split_ok", "xhigh_ok", "odd2_ok"))
        mask16_step = sem("mask16_step")
        wr_step, eprod2_ok, vprod2_ok = sem("wr_step"), sem("eprod2_ok"), sem("vprod2_ok")
        ew_ok, tg_ok, ek_ok, decay_ok, diag_ok = (sem(n) for n in ("ew_ok", "tg_ok", "ek_ok", "decay_ok", "diag_ok"))
        ekv_ok, scan_ok = sem("ekv_ok"), sem("scan_ok")
        kv_ps, kv_ok = sem("kv_ps"), sem("kv_ok")
        bn_ok, aggr_ok, ve_ok, rstd_ok, norm_ok = ([sem(f"{n}{i}") for i in range(5)] for n in (
            "bn_ok", "aggr_ok", "ve_ok", "rstd_ok", "norm_ok"))
        er_ok, mix_ps, dn_ok, rec_ok, mixed_ok, x1_ok = (
            sem(n) for n in ("er_ok", "mix_ps", "dn_ok", "rec_ok", "mixed_ok", "x1_ok"))
        turn_ps, xnT_ok, logit_ps, logit_ok = (sem(n) for n in ("turn_ps", "xnT_ok", "logit_ps", "logit_ok"))
        ch, egap_ok = sem("choose_step"), sem("egap_ok")
        rk, elig_ok, rank_ps = sem("rank_step"), sem("elig_ok"), sem("rank_ps")
        coef_ok, coefT_ps, coefT_ok = (
            sem(n) for n in ("coef_ok", "coefT_ps", "coefT_ok"))
        up_ps, up_ok, down_ps, sum_ok = (sem(n) for n in ("up_ps", "up_ok", "down_ps", "sum_ok"))
        T3_ps, T3_ok, q_ps, q_ok = (sem(n) for n in ("T3_ps", "T3_ok", "q_ps", "q_ok"))
        eprod_ok, ered_ok, max_ok, sub_ok, exp_ok, vprod_ok, soft_ok, rs_ok, vred_ok, att_ok = (
            sem(n) for n in ("eprod_ok", "ered_ok", "max_ok", "sub_ok", "exp_ok", "vprod_ok", "soft_ok", "rs_ok",
                             "vred_ok", "att_ok"))
        T4_ps, oT_ok, wo_ps, x3_ok, T5_ps, T5_ok = (
            sem(n) for n in ("T4_ps", "oT_ok", "wo_ps", "x3_ok", "T5_ps", "T5_ok"))
        fac_ps, fac_ok, up1_ps, hid1_ok, low_ps, low_ok, y_ps, y_ok, stored = (
            sem(n) for n in ("fac_ps", "fac_ok", "up1_ps", "hid1_ok", "low_ps", "low_ok", "y_ps", "y_ok", "stored"))

        def normalize(ops, i, tiles):
            for t in tiles:
                source, target = (att[:, t % 2, :], on[:, t, :]) if i == 3 else (x[:, t, :], xn[:, t, :])
                last = ops.tensor_scalar(target, source, mv[:, i, t, 0:1], rstd[:, i, t:t + 1],
                                         ALU.subtract, ALU.mult)
            last.then_inc(norm_ok[i], 1)

        def query_key_products(ops, eng, t, h0, h1, done):
            eng.wait_ge(q_ok, t + 1)
            eng.wait_ge(kv_ok, t + 1)
            if t >= 2:
                eng.wait_ge(ered_ok, t - 1)
            shape = [P, h1 - h0, NH, DH]
            qv = q_sb[:, t % 2, h0 * DH:h1 * DH].rearrange("p (h g d) -> p h g d", h=h1 - h0, g=1).broadcast_to(shape)
            kv = k_sb[:, t, :].rearrange("p (h g d) -> p h g d", h=1, g=NH).broadcast_to(shape)
            ops.tensor_tensor(eprod[t % 2].rearrange("p (h g d) -> p h g d", h=NH, g=NH)[:, h0:h1, :, :], qv, kv,
                              ALU.mult).then_inc(done, 1)

        def weight_value_products(ops, eng, t, h0, h1, done):
            eng.wait_ge(exp_ok, t + 1)
            if t >= 1:
                eng.wait_ge(vred_ok, t)
            shape = [P, h1 - h0, DH, NH]
            pv = pr[:, t % 2, h0:h1, :].unsqueeze(2).broadcast_to(shape)
            vv = v_sb[:, t, :].rearrange("p (h d g) -> p h d g", h=1, g=NH).broadcast_to(shape)
            ops.tensor_tensor(vprod.rearrange("p (h d g) -> p h d g", h=NH, d=DH)[:, h0:h1, :, :], pv, vv,
                              ALU.mult).then_inc(done, 1)

        block = ctx.enter_context(nc.Block())

        @block.sync
        def _(sp):
            sp.dma_start(ctxT_sb[:, :], ctxT).then_inc(ld_ctx, 16)
            sp.dma_start(col[:, :], cols).then_inc(ld_col, 16)
            sp.dma_start(x[:, :, :].rearrange("p b d -> p (b d)"), x_in).then_inc(ld_x, 16)
            sp.dma_start(sw[:, :], small).then_inc(ld_small, 16)
            sp.dma_start(row5[:, :], rows).then_inc(ld_row, 16)
            sp.dma_start(gate[:, :], gates.broadcast_to([P, 5])).then_inc(ld_gate, 16)
            for n, e in enumerate(FFNS[:NSTAGE]):
                sp.dma_start(w_stage[:, n, :], w_up[:, e, :]).then_inc(ld_up[e], 16)
            sp.wait_ge(row_step, 5)
            for i in range(3):
                sp.dma_start(row3[i:i + 1, :], row_part[:, i, :]).then_inc(row3_ok, 16)
            for n, e in enumerate(FFNS[NSTAGE:], NSTAGE):
                sp.wait_ge(split_ok, n - NSTAGE + 1)
                sp.dma_start(w_stage[:, n % NSTAGE, :], w_up[:, e, :]).then_inc(ld_up[e], 16)
            for e in FFNS:
                sp.dma_start(wd[:, e, :, :], w_down[:, e, :, :]).then_inc(ld_dn[e], 16)
            sp.dma_start(b2_sb[:, :], b2).then_inc(ld_b2, 16)
            sp.dma_start(w1u[:, :], l1_up).then_inc(ld_l1, 16)
            sp.dma_start(w1d[:, :, :], l1_down).then_inc(ld_l1, 16)
            for t in range(NB):
                sp.wait_ge(y_ok, t + 1)
                sp.dma_start(out[t, :, :], x[:, t, :]).then_inc(stored, 16)
            sp.wait_ge(stored, 16 * NB)

        @block.gpsimd
        def _(pool):
            nc.gpsimd.memset(ones_bf[:, :], 1.0).then_inc(zeroed, 1)
            nc.gpsimd.memset(decay[:, :], 1.0).then_inc(zeroed, 1)
            nc.gpsimd.memset(ident[:, :], 0.0).then_inc(zeroed, 1)
            nc.gpsimd.memset(minus_half[:, :], -0.5)
            pool.wait_ge(zeroed, 3)
            nc.gpsimd.affine_select(out=ident[:, :], in_=ident[:, :], compare_op=ALU.not_equal, fill=1.0, base=0,
                                    pattern=[[-1, P]], channel_multiplier=1).then_inc(consts, 1)
            pool.wait_ge(ew_ok, 1)
            pool.wait_ge(consts, 1)
            nc.gpsimd.tensor_scalar(diag_u[:, :], ident[:, :], ew[:, 1:2], None, ALU.mult).then_inc(diag_ok, 1)
            pool.wait_ge(masks, 1)
            for g in range(NG):
                pool.wait_ge(ek_ok, g + 1)
                nc.gpsimd.tensor_tensor(seg(src, 0, g, 1), seg(src, 1, g, 1),
                                        ctxT_sb[:, :].rearrange("p (b s) -> p b s", s=P)[:, g * GT:(g + 1) * GT, :],
                                        ALU.mult).then_inc(ekv_ok, 1)

            def root(i, a, b, count):
                pool.wait_ge(ve_ok[i], count)
                nc.gpsimd.tensor_tensor(rstd[:, i, a:b], ve[:, i, a:b], minus_half[:, 0:b - a],
                                        ALU.pow).then_inc(rstd_ok[i], 1)
                if i in POOL_NORMS:
                    pool.wait_ge(rstd_ok[i], count)
                    normalize(nc.gpsimd, i, range(a, b))

            root(0, 0, NB, 1)
            for name, *a in POOL_ORDER:
                if name == "constants":
                    nc.gpsimd.memset(ones3[:, :], 1.0)
                    nc.gpsimd.memset(pick[:, :, :], 0.0)
                    nc.gpsimd.memset(odd2[:, :, :], 0.0)
                    nc.gpsimd.memset(mask16[:, :, :], 0.0)
                    nc.gpsimd.memset(one8[:, :], 1.0)
                    nc.gpsimd.memset(mask_s[:, :, :], 0.0).then_inc(zeroed, 1)
                    pool.wait_ge(zeroed, 4)
                    nc.gpsimd.affine_select(out=tri[:, :], in_=ones_bf[:, :], compare_op=ALU.is_ge, fill=0.0, base=0,
                                            pattern=[[1, P]], channel_multiplier=-1)
                    nc.gpsimd.affine_select(out=mask_s[:, :, :], in_=mask_s[:, :, :], compare_op=ALU.not_equal,
                                            fill=1.0, base=0, pattern=[[-1, NL], [0, P]], channel_multiplier=1)
                    for r in range(FB):
                        nc.gpsimd.affine_select(out=mask16[:, :, :], in_=mask16[:, :, :], compare_op=ALU.not_equal,
                                                fill=1.0, base=-NL * r, pattern=[[-1, NL], [0, P // NL]],
                                                channel_multiplier=1).then_inc(mask16_step, 1)
                        pool.wait_ge(mask16_step, r + 1)
                    for r in range(FB):
                        nc.gpsimd.tensor_copy(pick[:, r, NL * r:NL * (r + 1)], ident[:, 1 + 2 * NL:1 + 4 * NL:2])
                    nc.gpsimd.iota(iota_e[:, :], [[1, NE]], base=0, channel_multiplier=0,
                                   allow_small_or_imprecise_dtypes=True).then_inc(consts, 1)
                elif name == "bias":
                    pool.wait_ge(ld_row, 16)
                    for i in range(3):
                        nc.gpsimd.tensor_copy(row_part[:, i, :], row5[:, :]).then_inc(row_step, 1)
                        if i < 2:
                            pool.wait_ge(row_step, 2 * i + 1)
                            nc.gpsimd.tensor_tensor(row5[:, :], row5[:, :], row_part[:, i, :],
                                                    ALU.subtract).then_inc(row_step, 1)
                            pool.wait_ge(row_step, 2 * i + 2)
                elif name == "mix":
                    g, = a
                    pool.wait_ge(mixed_ok, g + 1)
                    xg = x[:, g * GT:(g + 1) * GT, :].rearrange("p b d -> p (b d)")
                    nc.gpsimd.tensor_tensor(xg, xg, mixed[:, g % 2, :], ALU.add).then_inc(x1_ok, 1)
                elif name == "stat1":
                    root(1, GT * a[0], GT * a[0] + GT, a[0] + 1)
                elif name == "stat3":
                    root(2, a[0], a[0] + 1, a[0] + 1)
                elif name == "vsum":
                    root(3, a[0], a[0] + 1, a[0] + 1)
                elif name == "stat5":
                    root(4, a[0], a[0] + 1, a[0] + 1)
                elif name == "eprod":
                    query_key_products(nc.gpsimd, pool, a[0], 0, HEADS[a[0]], eprod_ok)
                elif name == "vprod":
                    weight_value_products(nc.gpsimd, pool, a[0], 0, HEADS[a[0]], vprod_ok)

        @block.scalar
        def _(act):
            act.wait_ge(ld_col, 16)
            nc.scalar.activation(ew[:, :], col[:, C_W:C_U + 1], ACT.Exp).then_inc(ew_ok, 1)
            act.wait_ge(ld_ctx, 16)
            for g in range(NG):
                nc.scalar.activation(seg(src, 1, g, 1),
                                     ctxT_sb[:, :].rearrange("p (b s) -> p b s", s=P)[:, g * GT:(g + 1) * GT, :],
                                     ACT.Exp).then_inc(ek_ok, 1)
            act.wait_ge(ld_small, 16)
            nc.scalar.activation(wr[:, 0, :], sw[:, S_R:S_R + NE], ACT.Copy, scale=S_WT).then_inc(wr_step, 1)
            act.wait_ge(ld_gate, 16)
            nc.scalar.activation(tg[:, :], gate[:, 0:4], ACT.Tanh).then_inc(tg_ok, 1)
            act.wait_ge(norm_ok[0], 1)
            for t in range(NB):
                nc.scalar.activation(on[:, t, :], x[:, t, :], ACT.Exp, scale=neg_rstd[:, t:t + 1],
                                     bias=mu_rstd[:, t:t + 1]).then_inc(er_ok, 1)
            for name, *a in ACT_ORDER:
                if name == "split":
                    act.wait_ge(ld_up[a[0]], 16)
                    nc.scalar.activation(wu[:, 0, a[0], :], w_stage[:, FFNS.index(a[0]) % NSTAGE, :], ACT.Copy,
                                         scale=S_WT).then_inc(high_ok, 1)
                elif name == "kv":
                    for t in range(a[0] * GT, a[0] * GT + GT):
                        act.wait_ge(kv_ps, t + 1)
                        nc.scalar.copy(k_sb[:, t, :], work_bank("kv", t)[:, 0:D])
                        nc.scalar.copy(v_sb[:, t, :], work_bank("kv", t)[:, D:2 * D]).then_inc(kv_ok, 1)
                elif name == "rows":
                    g, = a
                    act.wait_ge(turn_ps, g + 1)
                    nc.scalar.activation(xnT[:, 0, g * GT:(g + 1) * GT, :].rearrange("p b t -> p (b t)"),
                                         ps_turn[:, 0:GT * P], ACT.Copy, scale=S_X).then_inc(xhigh_ok, 1)
                elif name == "turn":
                    g, = a
                    act.wait_ge(coefT_ps, g + 1)
                    nc.scalar.copy(coefT[:, g * GT:(g + 1) * GT, :].rearrange("p b t -> p (b t)"),
                                   ps_turn[0:NF, 0:GT * P]).then_inc(coefT_ok, 1)
                elif name == "choose2":
                    act.wait_ge(ch, 3)
                    nc.scalar.activation(egap[:, :], gap[:, :], ACT.Exp).then_inc(egap_ok, 1)
                elif name == "up":
                    g, e, i = a
                    n = NTH_UP[g, e] * PAIRS + i
                    act.wait_ge(up_ps, n + 1)
                    if g >= 2:
                        act.wait_ge(down_ps, TERMS.index((g * GT - GT - 1, e)) // CHUNK + 1)
                    for k in range(2):
                        j = 2 * i + k
                        last = nc.scalar.activation(hid[:, g % 2, e, j, :],
                                                    work_bank("up", g, e, i)[:, k * GT * P:(k + 1) * GT * P],
                                                    ACT.Gelu, bias=col[:, C_B1 + e * FB + j:C_B1 + e * FB + j + 1],
                                                    scale=1.0 / (S_X * S_WT))
                    last.then_inc(up_ok, 1)
                elif name == "turn3":
                    t, = a
                    act.wait_ge(T3_ps, t + 1)
                    if t >= 2:
                        act.wait_ge(q_ps, t - 1)
                    nc.scalar.copy(xT3[:, t % 2, :], T3).then_inc(T3_ok, 1)
                elif name == "query":
                    t, = a
                    act.wait_ge(q_ps, t + 1)
                    if t >= 2:
                        act.wait_ge(eprod_ok, t - 1)
                        act.wait_ge(eprod2_ok, t - 1)
                    nc.scalar.copy(q_sb[:, t % 2, :], Q).then_inc(q_ok, 1)
                elif name == "esum":
                    t, = a
                    act.wait_ge(sub_ok, t + 1)
                    if t >= 2:
                        act.wait_ge(vprod_ok, t - 1)
                        act.wait_ge(vprod2_ok, t - 1)
                        act.wait_ge(soft_ok, t - 1)
                    nc.scalar.activation(pr[:, t % 2, :, :], en[:, t % 2, :, :], ACT.Exp,
                                         scale=INV_SQRT_D).then_inc(exp_ok, 1)
                elif name == "turn4":
                    t, = a
                    act.wait_ge(T4_ps, t + 1)
                    if t >= 2:
                        act.wait_ge(wo_ps, t - 1)
                    nc.scalar.activation(oT[:, t % 2, :], T4, ACT.Identity, scale=col[:, C_LNG:C_LNG + 1],
                                         bias=col[:, C_LNB:C_LNB + 1]).then_inc(oT_ok, 1)
                elif name == "turn5":
                    t, = a
                    act.wait_ge(T5_ps, t + 1)
                    if t >= 2:
                        act.wait_ge(low_ps, t - 1)
                    nc.scalar.copy(xT5[:, t % 2, :], T5).then_inc(T5_ok, 1)
                elif name == "up1":
                    t, = a
                    act.wait_ge(up1_ps, t + 1)
                    if t >= 2:
                        act.wait_ge(y_ps, t - 1)
                    for j in range(FB):
                        last = nc.scalar.activation(hid1[:, t % 2, j, :], ps_h1[:, j * P:(j + 1) * P], ACT.Gelu,
                                                    bias=col[:, C_L1B1 + j:C_L1B1 + j + 1])
                    last.then_inc(hid1_ok, 1)
                elif name == "low2":
                    t, = a
                    act.wait_ge(low_ps, t + 1)
                    if t >= 2:
                        act.wait_ge(y_ps, t - 1)
                    nc.scalar.copy(low[:, t % 2, :], ps_h1[0:FB * NL, 0:P]).then_inc(low_ok, 1)

        @block.vector
        def _(dve):
            def stats(i, tiles, source, ready, count):
                if ready is not None:
                    dve.wait_ge(ready, count)
                for t in tiles:
                    last = nc.vector.bn_stats(bn[:, t, :], source(t))
                last.then_inc(bn_ok[i], 1)
                call = tiles[0] // len(tiles) + 1
                dve.wait_ge(bn_ok[i], call)
                for t in tiles:
                    last = nc.vector.bn_aggr(mv[:, i, t, :], bn[:, t, :])
                last.then_inc(aggr_ok[i], 1)
                dve.wait_ge(aggr_ok[i], call)
                a, b = tiles[0], tiles[-1] + 1
                nc.vector.tensor_scalar(ve[:, i, a:b], mv[:, i, a:b, 1], EPS, None, ALU.add).then_inc(ve_ok[i], 1)

            def norm(i, tiles):
                if i not in POOL_NORMS:
                    dve.wait_ge(rstd_ok[i], tiles[0] // len(tiles) + 1)
                    normalize(nc.vector, i, tiles)

            def x_tile(t):
                return x[:, t, :]

            nc.vector.memset(src[:, :, 0:SCAN:SEG], 0.0).then_inc(masks, 1)
            nc.vector.memset(live[:, :], 1.0)
            nc.vector.memset(before[:, :, 0:1], 0.0).then_inc(masks, 1)
            dve.wait_ge(zeroed, 2)
            nc.vector.memset(decay[:, 0:SCAN:SEG], 0.0).then_inc(masks, 1)
            dve.wait_ge(masks, 3)
            dve.wait_ge(ew_ok, 1)
            nc.vector.tensor_scalar(decay[:, :], decay[:, :], ew[:, 0:1], None, ALU.mult).then_inc(decay_ok, 1)
            dve.wait_ge(decay_ok, 1)

            def scans(g):
                dve.wait_ge(ek_ok, g + 1)
                a, b = g * GT * SEG, (g + 1) * GT * SEG
                back = slice(b, a, -1)
                for s in (1, 0):
                    if s == 0:
                        dve.wait_ge(ekv_ok, g + 1)
                    nc.vector.tensor_tensor_scan(fwd[:, s, a:b], decay[:, a:b], src[:, s, a:b], 0.0,
                                                 ALU.mult, ALU.add)
                    last = nc.vector.tensor_tensor_scan(bwd[:, s, back], decay[:, back], src[:, s, back], 0.0,
                                                        ALU.mult, ALU.add)
                last.then_inc(scan_ok, 1)

            def mixer(g):
                ts = slice(g * GT, (g + 1) * GT)
                m = mixed[:, g % 2, :]
                dve.wait_ge(mix_ps, g + 1)
                dve.wait_ge(er_ok, (g + 1) * GT)
                dve.wait_ge(tg_ok, 1)
                if g >= 2:
                    dve.wait_ge(x1_ok, g - 1)
                nc.vector.scalar_tensor_tensor(m, on[:, ts, :].rearrange("p b d -> p (b d)"), 1.0,
                                               ps_mix[g % 2][:, GT * D:2 * GT * D], ALU.add, ALU.mult).then_inc(dn_ok, 1)
                dve.wait_ge(dn_ok, g + 1)
                nc.vector.reciprocal(m, m).then_inc(rec_ok, 1)
                dve.wait_ge(rec_ok, g + 1)
                nc.vector.scalar_tensor_tensor(m, ps_mix[g % 2][:, 0:GT * D], tg[:, G_X0:G_X0 + 1], m,
                                               ALU.mult, ALU.mult).then_inc(mixed_ok, 1)

            scans(0)
            dve.wait_ge(ld_x, 16)
            stats(0, list(range(NB)), x_tile, None, 0)
            scans(1)
            dve.wait_ge(rstd_ok[0], 1)
            nc.vector.tensor_scalar(neg_rstd[:, :], rstd[:, 0, :], -1.0, None, ALU.mult)
            nc.vector.tensor_tensor(mu_rstd[:, :], rstd[:, 0, :], mv[:, 0, :, 0], ALU.mult).then_inc(norm_ok[0], 1)
            dve.wait_ge(wr_step, 1)
            nc.vector.scalar_tensor_tensor(wr[:, 1, :], sw[:, S_R:S_R + NE], S_WT, wr[:, 0, :],
                                           ALU.mult, ALU.subtract).then_inc(wr_step, 1)
            for name, *a in DVE_ORDER:
                if name == "mix":
                    mixer(a[0])
                elif name == "split":
                    n = FFNS.index(a[0])
                    dve.wait_ge(high_ok, n + 1)
                    nc.vector.scalar_tensor_tensor(wu[:, 1, a[0], :], w_stage[:, n % NSTAGE, :], S_WT,
                                                   wu[:, 0, a[0], :], ALU.mult, ALU.subtract).then_inc(split_ok, 1)
                elif name == "scan" and a[0] >= 2:
                    scans(a[0])
                elif name == "stat1":
                    g, = a
                    stats(1, list(range(g * GT, g * GT + GT)), x_tile, x1_ok, g + 1)
                elif name == "rows":
                    g, = a
                    norm(1, range(g * GT, g * GT + GT))
                elif name == "xlow":
                    g, = a
                    dve.wait_ge(xhigh_ok, g + 1)
                    nc.vector.scalar_tensor_tensor(
                        xnT[:, 1, g * GT:(g + 1) * GT, :].rearrange("p b t -> p (b t)"), ps_turn[:, 0:GT * P], S_X,
                        xnT[:, 0, g * GT:(g + 1) * GT, :].rearrange("p b t -> p (b t)"),
                        ALU.mult, ALU.subtract).then_inc(xnT_ok, 1)
                elif name == "choose":
                    dve.wait_ge(logit_ps, NG)
                    nc.vector.tensor_scalar(logit[:, :, :].rearrange("p b e -> p (b e)"), ps_logit[:, 0:NB * NE],
                                            1.0 / (S_X * S_WT), None, ALU.mult).then_inc(logit_ok, 1)
                    dve.wait_ge(logit_ok, 1)
                    for t in range(NB):
                        last = nc.vector.max(top[:, t, :], logit[:, t, :])
                    last.then_inc(ch, 1)
                    dve.wait_ge(ch, 1)
                    for t in range(NB):
                        last = nc.vector.max_index(topi[:, t, :], top[:, t, :], logit[:, t, :])
                    last.then_inc(ch, 1)
                    nc.vector.tensor_tensor(gap[:, :], top[:, :, 1], top[:, :, 0], ALU.subtract).then_inc(ch, 1)
                    dve.wait_ge(ch, 3)
                    nc.vector.tensor_copy(topf[:, :, :], topi[:, :, 0:2]).then_inc(ch, 1)
                    dve.wait_ge(ch, 4)
                    dve.wait_ge(consts, 2)
                    for i in range(2):
                        last = nc.vector.tensor_tensor(
                            hot[:, i, :, :], iota_e[:, :].unsqueeze(1).broadcast_to([P, NB, NE]),
                            topf[:, :, i:i + 1].broadcast_to([P, NB, NE]), ALU.is_equal)
                    last.then_inc(ch, 1)
                    dve.wait_ge(ch, 5)
                    nc.vector.tensor_tensor(assign[:, :, :], hot[:, 0, :, :], hot[:, 1, :, :],
                                            ALU.add).then_inc(ch, 1)
                elif name == "choose2":
                    dve.wait_ge(egap_ok, 1)
                    nc.vector.tensor_scalar(den2[:, :], egap[:, :], 1.0, None, ALU.add).then_inc(ch, 1)
                    dve.wait_ge(ch, 7)
                    nc.vector.reciprocal(wt[:, 0, :], den2[:, :]).then_inc(ch, 1)
                    dve.wait_ge(ch, 8)
                    nc.vector.tensor_tensor(wt[:, 1, :], wt[:, 0, :], egap[:, :], ALU.mult).then_inc(ch, 1)
                    dve.wait_ge(ch, 9)
                    for i in range(2):
                        last = nc.vector.tensor_tensor(
                            hot[:, i, :, :], hot[:, i, :, :],
                            wt[:, i, :].unsqueeze(2).broadcast_to([P, NB, NE]), ALU.mult)
                    last.then_inc(ch, 1)
                    dve.wait_ge(ch, 10)
                    nc.vector.tensor_tensor(weight[:, :, :], hot[:, 0, :, :], hot[:, 1, :, :],
                                            ALU.add).then_inc(ch, 1)
                    dve.wait_ge(ch, 11)
                    dve.wait_ge(tg_ok, 1)
                    nc.vector.tensor_scalar(weight[:, :, :], weight[:, :, :], tg[:, G_F0:G_F0 + 1], None,
                                            ALU.mult).then_inc(ch, 1)
                    dve.wait_ge(ch, 12)
                elif name == "rank":
                    e, = a
                    dve.wait_ge(rk, 2 * e) if e else dve.wait_ge(masks, 3)
                    if e == 0:
                        dve.wait_ge(ch, 6)
                    nc.vector.tensor_tensor(elig[:, e, :], assign[:, :, e], live[:, :], ALU.mult).then_inc(elig_ok, 1)
                    dve.wait_ge(elig_ok, 2 * e + 1)
                    nc.vector.tensor_tensor_scan(before[:, e, 1:NB + 1], one8[:, :], elig[:, e, :], 0.0,
                                                 ALU.mult, ALU.add).then_inc(elig_ok, 1)
                    dve.wait_ge(rank_ps, e + 1)
                    nc.vector.scalar_tensor_tensor(over[:, :], ps_rank[:, e * NB:(e + 1) * NB],
                                                   float(CAP), elig[:, e, :], ALU.is_gt, ALU.mult).then_inc(rk, 1)
                    dve.wait_ge(rk, 2 * e + 1)
                    nc.vector.tensor_tensor(live[:, :], live[:, :], over[:, :], ALU.subtract).then_inc(rk, 1)
                elif name == "coef":
                    dve.wait_ge(rk, 2 * NE)
                    nc.vector.tensor_tensor(coef[:, :, 0:NE], weight[:, :, :],
                                            live[:, :].unsqueeze(2).broadcast_to([P, NB, NE]), ALU.mult)
                    nc.vector.tensor_scalar(over[:, :], live[:, :], -1.0, 1.0, ALU.mult, ALU.add).then_inc(rk, 1)
                    dve.wait_ge(rk, 2 * NE + 1)
                    nc.vector.tensor_scalar(coef[:, :, FALL], over[:, :], tg[:, G_F0:G_F0 + 1], None,
                                            ALU.mult).then_inc(coef_ok, 1)
                elif name == "down":
                    c, = a
                    dve.wait_ge(down_ps, c + 1)
                    dve.wait_ge(coef_ok, 1)
                    for n in range(c * CHUNK, (c + 1) * CHUNK):
                        t, e = TERMS[n]
                        if n:
                            dve.wait_ge(sum_ok, n)
                        nc.vector.scalar_tensor_tensor(x[:, t, :], place(n),
                                                       1.0 if e is None else coef[:, t, e:e + 1], x[:, t, :],
                                                       ALU.mult, ALU.add).then_inc(sum_ok, 1)
                elif name == "stat3":
                    t, = a
                    stats(2, [t], x_tile, sum_ok, NTERM * (t + 1))
                elif name == "norm3":
                    norm(2, [a[0]])
                elif name == "eprod":
                    query_key_products(nc.vector, dve, a[0], HEADS[a[0]], NH, eprod2_ok)
                elif name == "vprod":
                    weight_value_products(nc.vector, dve, a[0], HEADS[a[0]], NH, vprod2_ok)
                elif name == "esum":
                    t, = a
                    dve.wait_ge(eprod_ok, t + 1)
                    dve.wait_ge(eprod2_ok, t + 1)
                    if t >= 2:
                        dve.wait_ge(exp_ok, t - 1)
                    e2 = en[:, t % 2, :, :]
                    nc.vector.tensor_reduce(e2.rearrange("p h g -> p (h g)"),
                                            eprod[t % 2].rearrange("p (e d) -> p e d", d=DH), AX_X,
                                            ALU.add).then_inc(ered_ok, 1)
                    dve.wait_ge(ered_ok, t + 1)
                    nc.vector.tensor_reduce(mx[:, t % 2, :], e2, AX_X, ALU.max).then_inc(max_ok, 1)
                    dve.wait_ge(max_ok, t + 1)
                    nc.vector.tensor_tensor(e2, e2, mx[:, t % 2, :].unsqueeze(2).broadcast_to([P, NH, NH]),
                                            ALU.subtract).then_inc(sub_ok, 1)
                elif name == "soft":
                    t, = a
                    dve.wait_ge(exp_ok, t + 1)
                    nc.vector.tensor_reduce(sm[:, t % 2, :], pr[:, t % 2, :, :], AX_X, ALU.add).then_inc(soft_ok, 1)
                    dve.wait_ge(soft_ok, t + 1)
                    nc.vector.reciprocal(rs[:, t % 2, :], sm[:, t % 2, :]).then_inc(rs_ok, 1)
                elif name == "vsum":
                    t, = a
                    dve.wait_ge(vprod_ok, t + 1)
                    dve.wait_ge(vprod2_ok, t + 1)
                    if t >= 2:
                        dve.wait_ge(norm_ok[3], t - 1)
                    nc.vector.tensor_reduce(att[:, t % 2, :], vprod.rearrange("p (e g) -> p e g", g=NH), AX_X,
                                            ALU.add).then_inc(vred_ok, 1)
                    dve.wait_ge(vred_ok, t + 1)
                    dve.wait_ge(rs_ok, t + 1)
                    av = att[:, t % 2, :].rearrange("p (h d) -> p h d", d=DH)
                    nc.vector.tensor_tensor(av, av, rs[:, t % 2, :].unsqueeze(2).broadcast_to([P, NH, DH]),
                                            ALU.mult).then_inc(att_ok, 1)
                    stats(3, [t], lambda t: att[:, t % 2, :], att_ok, t + 1)
                elif name == "norm4":
                    norm(3, [a[0]])
                elif name == "wo":
                    t, = a
                    dve.wait_ge(wo_ps, t + 1)
                    nc.vector.scalar_tensor_tensor(x[:, t, :], WO, tg[:, G_X1:G_X1 + 1], x[:, t, :],
                                                   ALU.mult, ALU.add).then_inc(x3_ok, 1)
                elif name == "stat5":
                    stats(4, [a[0]], x_tile, x3_ok, a[0] + 1)
                elif name == "norm5":
                    norm(4, [a[0]])
                elif name == "lora":
                    t, = a
                    if t == 0:
                        dve.wait_ge(ld_gate, 16)
                        nc.vector.tensor_scalar(mask_s[:, :, :], mask_s[:, :, :],
                                                gate[0:NL, G_SCALE:G_SCALE + 1], None, ALU.mult).then_inc(mask_ok, 1)
                        nc.vector.tensor_scalar(mask16[:, :, :], mask16[:, :, :],
                                                gate[0:FB * NL, G_SCALE:G_SCALE + 1], None,
                                                ALU.mult).then_inc(mask_ok, 1)
                        dve.wait_ge(mask_ok, 2)
                    if t >= 2:
                        dve.wait_ge(y_ps, t - 1)
                    dve.wait_ge(T5_ok, t + 1)
                    nc.vector.tensor_copy(
                        odd2[:, t % 2, :].rearrange("p (r s) -> p r s", r=FB)[:, :, 0:NL],
                        xT5[:, t % 2, 2 + 2 * NL:2 + 4 * NL:2].unsqueeze(1).broadcast_to([P, FB, NL])
                        ).then_inc(odd2_ok, 1)
                    dve.wait_ge(fac_ps, t + 1)
                    nc.vector.tensor_copy(even1[:, t % 2, :], EVEN1)
                    nc.vector.tensor_tensor(u_mask[:, t % 2, :, :], U1.unsqueeze(1).broadcast_to([NL, NL, P]),
                                            mask_s[:, :, :], ALU.mult)
                    nc.vector.tensor_tensor(even2[:, t % 2, :, :],
                                            EVEN2.unsqueeze(1).broadcast_to([FB * NL, NL, P // NL]),
                                            mask16[:, :, :], ALU.mult).then_inc(fac_ok, 1)
                elif name == "down1":
                    t, = a
                    dve.wait_ge(y_ps, t + 1)
                    nc.vector.scalar_tensor_tensor(x[:, t, :], Y5, tg[:, G_F1:G_F1 + 1], x[:, t, :],
                                                   ALU.mult, ALU.add).then_inc(y_ok, 1)

        @block.tensor
        def _(pe):
            mm = nc.tensor.matmul

            def bank_free(*item):
                n = WORK.index(item) - NWORK
                if n < 0:
                    return
                kind, *b = WORK[n]
                if kind == "kv":
                    pe.wait_ge(kv_ok, b[0] + 1)
                elif kind == "up":
                    pe.wait_ge(up_ok, NTH_UP[b[0], b[1]] * PAIRS + b[2] + 1)
                else:
                    pe.wait_ge(sum_ok, (b[0] + 1) * CHUNK)

            def project(dst, lhsT, w0, r0, n):
                mm(dst, lhsT, sw[:, w0:w0 + n], start=True, stop=False)
                return mm(dst, ones3[:, :], row3[:, r0:r0 + n], start=False, stop=True)

            def three(dst, parts_a, parts_b):
                mm(dst, parts_a[0], parts_b[0], start=True, stop=False)
                mm(dst, parts_a[0], parts_b[1], start=False, stop=False)
                return mm(dst, parts_a[1], parts_b[0], start=False, stop=True)

            for name, *a in PE_ORDER:
                if name == "kv":
                    if a[0] == 0:
                        pe.wait_ge(ld_ctx, 16)
                        pe.wait_ge(ld_small, 16)
                        pe.wait_ge(row3_ok, 48)
                        pe.wait_ge(consts, 2)
                    for t in range(a[0] * GT, a[0] * GT + GT):
                        bank_free("kv", t)
                        project(work_bank("kv", t)[:, 0:2 * D], ctxT_sb[:, t * P:(t + 1) * P], S_KV, R_KV,
                                2 * D).then_inc(kv_ps, 1)
                elif name == "mix":
                    g, = a
                    pe.wait_ge(scan_ok, g + 1)
                    pe.wait_ge(diag_ok, 1)
                    if g >= 2:
                        pe.wait_ge(mixed_ok, g - 1)
                    for s in (1, 0):
                        for i in range(GT):
                            o = (g * GT + i) * SEG
                            d = ps_mix[g % 2][:, (s * GT + i) * D:(s * GT + i + 1) * D]
                            mm(d, fwd[:, s, o:o + P], ident[:, :], start=True, stop=False)
                            mm(d, bwd[:, s, o + 2:o + 2 + P], ident[:, :], start=False, stop=False)
                            last = mm(d, src[:, s, o + 1:o + 1 + P], diag_u[:, :], start=False, stop=True)
                    last.then_inc(mix_ps, 1)
                elif name == "rows":
                    g, = a
                    pe.wait_ge(norm_ok[1], g + 1)
                    if g:
                        pe.wait_ge(xnT_ok, g)
                    for i in range(GT):
                        last = nc.tensor.transpose(ps_turn[:, i * P:(i + 1) * P], xn[:, g * GT + i, :], ident[:, :])
                    last.then_inc(turn_ps, 1)
                elif name == "logits":
                    g, = a
                    pe.wait_ge(xnT_ok, g + 1)
                    pe.wait_ge(wr_step, 2)
                    for t in range(g * GT, g * GT + GT):
                        last = three(ps_logit[:, t * NE:(t + 1) * NE], (xnT[:, 0, t, :], xnT[:, 1, t, :]),
                                     (wr[:, 0, :], wr[:, 1, :]))
                    last.then_inc(logit_ps, 1)
                elif name == "rank":
                    e, = a
                    d = ps_rank[:, e * NB:(e + 1) * NB]
                    pe.wait_ge(elig_ok, 2 * e + 2)
                    mm(d, tri[:, :], elig[:, e, :], start=True, stop=False)
                    mm(d, ones_bf[:, :], before[:, e, 0:NB], start=False, stop=True).then_inc(rank_ps, 1)
                elif name == "turn":
                    g, = a
                    pe.wait_ge(coef_ok, 1)
                    pe.wait_ge(coefT_ok, g) if g else pe.wait_ge(xnT_ok, NG)
                    for i in range(GT):
                        last = nc.tensor.transpose(ps_turn[0:NF, i * P:(i + 1) * P], coef[:, g * GT + i, :],
                                                   ident[:, :])
                    last.then_inc(coefT_ps, 1)
                elif name == "up":
                    g, e, i = a
                    if i == 0:
                        pe.wait_ge(split_ok, FFNS.index(e) + 1)
                        pe.wait_ge(xnT_ok, g + 1)
                    bank_free("up", g, e, i)
                    ts = slice(g * GT, (g + 1) * GT)
                    rows = [xnT[:, k, ts, :].rearrange("p b t -> p (b t)") for k in range(2)]
                    for k in range(2):
                        c = slice((2 * i + k) * P, (2 * i + k + 1) * P)
                        last = three(work_bank("up", g, e, i)[:, k * GT * P:(k + 1) * GT * P],
                                     (wu[:, 0, e, c], wu[:, 1, e, c]), rows)
                    last.then_inc(up_ps, 1)
                elif name == "down":
                    c, = a
                    bank_free("down", c)
                    for n in range(c * CHUNK, (c + 1) * CHUNK):
                        t, e = TERMS[n]
                        if e is None:
                            pe.wait_ge(ld_b2, 16)
                            pe.wait_ge(coefT_ok, t // GT + 1)
                            last = mm(place(n), coefT[:, t, :], b2_sb[:, :], start=True, stop=True)
                            continue
                        pe.wait_ge(ld_dn[e], 16)
                        pe.wait_ge(up_ok, (NTH_UP[t // GT, e] + 1) * PAIRS)
                        for j in range(FB):
                            last = mm(place(n), hid[:, t // GT % 2, e, j, t % GT * P:(t % GT + 1) * P], wd[:, e, j, :],
                                      start=(j == 0), stop=(j == FB - 1))
                    last.then_inc(down_ps, 1)
                elif name == "turn3":
                    t, = a
                    pe.wait_ge(norm_ok[2], t + 1)
                    if t:
                        pe.wait_ge(q_ok, t)
                    nc.tensor.transpose(T3, xn[:, t, :], ident[:, :]).then_inc(T3_ps, 1)
                elif name == "query":
                    t, = a
                    pe.wait_ge(T3_ok, t + 1)
                    project(Q, xT3[:, t % 2, :], S_Q, R_Q, D).then_inc(q_ps, 1)
                elif name == "turn4":
                    t, = a
                    pe.wait_ge(norm_ok[3], t + 1)
                    if t:
                        pe.wait_ge(x3_ok, t)
                    nc.tensor.transpose(T4, on[:, t, :], ident[:, :]).then_inc(T4_ps, 1)
                elif name == "wo":
                    t, = a
                    pe.wait_ge(oT_ok, t + 1)
                    project(WO, oT[:, t % 2, :], S_O, R_O, D).then_inc(wo_ps, 1)
                elif name == "turn5":
                    t, = a
                    pe.wait_ge(norm_ok[4], t + 1)
                    pe.wait_ge(fac_ok, t) if t else pe.wait_ge(coefT_ok, NG)
                    nc.tensor.transpose(T5, xn[:, t, :], ident[:, :]).then_inc(T5_ps, 1)
                elif name == "lora":
                    t, = a
                    pe.wait_ge(T5_ok, t + 1)
                    nc.tensor.transpose(EVEN1, xT5[:, t % 2, 1:1 + 2 * NL:2], ident[:, :])
                    for r in range(FB):
                        mm(EVEN2, pick[:, r, :], xn[:, t, r:D:FB], start=(r == 0), stop=(r == FB - 1))
                    mm(U1, xT5[:, t % 2, 2:2 + 2 * NL:2], xT5[:, t % 2, :],
                       start=True, stop=True).then_inc(fac_ps, 1)
                elif name == "up1":
                    t, = a
                    pe.wait_ge(fac_ok, t + 1)
                    pe.wait_ge(ld_l1, 32)
                    if t:
                        pe.wait_ge(low_ok, t)
                    for j in range(FB):
                        d = ps_h1[:, j * P:(j + 1) * P]
                        mm(d, w1u[:, j * P:(j + 1) * P], xT5[:, t % 2, :], start=True, stop=False)
                        last = mm(d, even1[:, t % 2, :], u_mask[:, t % 2, j, :], start=False, stop=True)
                    last.then_inc(up1_ps, 1)
                elif name == "low2":
                    t, = a
                    pe.wait_ge(hid1_ok, t + 1)
                    pe.wait_ge(odd2_ok, t + 1)
                    for r in range(FB):
                        last = mm(ps_h1[0:FB * NL, 0:P], odd2[:, t % 2, r * FB * NL:(r + 1) * FB * NL],
                                  hid1[:, t % 2, r, :], start=(r == 0), stop=(r == FB - 1))
                    last.then_inc(low_ps, 1)
                elif name == "down1":
                    t, = a
                    pe.wait_ge(low_ok, t + 1)
                    if t:
                        pe.wait_ge(y_ok, t)
                    for r in range(FB):
                        mm(Y5, hid1[:, t % 2, r, :], w1d[:, r, :], start=(r == 0), stop=False)
                    mm(Y5, low[:, t % 2, :], even2[:, t % 2, :, :].rearrange("p j o -> p (j o)"),
                       start=False, stop=False)
                    mm(Y5, ones3[:, :], row3[:, R_B2:R_B2 + D], start=False, stop=True).then_inc(y_ps, 1)


def kernel(**inputs):
    import numpy as np
    import concourse.bacc as bacc
    from concourse.bass_utils import run_bass_kernel_spmd

    a = {k: np.asarray(v) for k, v in inputs.items()}

    def hidden_cols(b):
        return b.reshape(-1, P).T

    w_up = np.concatenate([a["L0_ffn_W1"], a["L0_ffn_fw1"][None]]).transpose(1, 0, 2)
    w_down = np.concatenate([a["L0_ffn_W2"], a["L0_ffn_fw2"][None]]).reshape(NF, FB, P, D).transpose(2, 0, 1, 3)
    by_dim = a["L1_xattn_Wv"].reshape(NH, DH, D).transpose(1, 0, 2).reshape(D, D)
    arrays = {
        "ctxT": a["ctx_1024"].transpose(2, 0, 1).reshape(D, NB * P),
        "x_in": a["x"].transpose(1, 0, 2).reshape(P, NB * D),
        "cols": np.concatenate([a["L0_xattn_w"].reshape(D, 1), a["L0_xattn_u"].reshape(D, 1),
                                a["L1_xattn_ln_g"].reshape(D, 1), a["L1_xattn_ln_b"].reshape(D, 1),
                                hidden_cols(a["L0_ffn_b1"]), hidden_cols(a["L0_ffn_fb1"]),
                                hidden_cols(a["L1_ffn_b1"])], axis=1),
        "gates": np.stack([a["g_xattn"][0], a["g_ffn"][0], a["g_xattn"][1], a["g_ffn"][1],
                           a["L1_ffn_scale"]]).reshape(1, 5),
        "rows": np.concatenate([a["L1_xattn_bk"], a["L1_xattn_bv"].reshape(NH, DH).T.reshape(D), a["L1_xattn_bq"],
                                a["L1_xattn_bo"], a["L1_ffn_b2"]]).reshape(NROW // D, D),
        "small": np.concatenate([a["L1_xattn_Wk"].T, by_dim.T, a["L1_xattn_Wq"].T, a["L1_xattn_Wo"].T,
                                 a["L0_ffn_Wr"]], axis=1),
        "w_up": w_up,
        "w_down": w_down,
        "b2": np.concatenate([a["L0_ffn_b2"], a["L0_ffn_fb2"][None]]),
        "l1_up": a["L1_ffn_W1"].T,
        "l1_down": a["L1_ffn_W2"].T.reshape(FB, P, D).transpose(1, 0, 2),
    }
    arrays = {k: np.ascontiguousarray(v) for k, v in arrays.items()}
    nc = bacc.Bacc("TRN2", target_bir_lowering=False, num_devices=1)
    aps = [nc.dram_tensor(k, v.shape, mybir.dt.from_np(v.dtype), kind="ExternalInput").ap()
           for k, v in arrays.items()]
    out = nc.dram_tensor("out", (NB, P, D), F32, kind="ExternalOutput").ap()
    flamingo_kernel(nc, *aps, out)
    r = run_bass_kernel_spmd(nc, [arrays], core_ids=[0])
    return r.results[0]["out"]
```
